# Optimizing a Trainium2 kernel written in Bass

```python
import numpy as np
import jax
import jax.numpy as jnp

def _softmax(x, axis=-1):
    return jax.nn.softmax(x, axis=axis)

def _gelu(x):
    return jax.nn.gelu(x, approximate=True)

def _silu(x):
    return jax.nn.silu(x)

def _sigmoid(x):
    return jax.nn.sigmoid(x)

def _layernorm(x, axis=-1, eps=1e-05):
    m = jnp.mean(x, axis=axis, keepdims=True)
    v = jnp.var(x, axis=axis, keepdims=True)
    return (x - m) / jnp.sqrt(v + eps)

def _scatter_add(tgt, idx, src, axis=0):
    return tgt.at[idx].add(src)

def _segment_sum(src, seg, n):
    return jax.ops.segment_sum(src, seg, n)
kernel_name = 'mk_xattn_ffn_d1_seqx_r8_66aba0'

def setup_inputs(seed: int=0):
    np.random.seed(seed)
    _w = jnp.asarray

    def _rec_inputs():
        import jax
        import jax.numpy as jnp
        _rk = jax.random.key(seed)
        x = 7.22e-05 + 1 * jax.random.normal(jax.random.fold_in(_rk, 1), (32, 128, 128), jnp.float32)
        _lenS = 128 - jax.random.randint(jax.random.fold_in(_rk, 7), (32,), 0, max(1, 128 // 4) + 1, jnp.int32)
        _lenS2 = 128 - jax.random.randint(jax.random.fold_in(_rk, 8), (32,), 0, max(1, 128 // 4) + 1, jnp.int32)
        _ctx_1024P = jax.random.normal(jax.random.fold_in(_rk, 11), (32, 16, 128), jnp.float32)
        _ctx_1024c = jax.random.dirichlet(jax.random.fold_in(_rk, 511), 0.3 * jnp.ones((16,), jnp.float32), (32, 128))
        _ctx_1024t = jnp.einsum('bsk,bkd->bsd', _ctx_1024c, _ctx_1024P)
        _ctx_1024t = _ctx_1024t * jax.lax.rsqrt(jnp.mean(jnp.square(_ctx_1024t)) + 1e-12) * 0.953939
        ctx_1024 = 4.13588e-05 + 0.999923 * (_ctx_1024t + 0.3 * jax.random.normal(jax.random.fold_in(_rk, 611), (32, 128, 128), jnp.float32))
        return (x, ctx_1024)
    x, ctx_1024 = _rec_inputs()

    def _L0_xattn_setup():
        import jax, jax.numpy as jnp
        import numpy as np
        N_HEADS = 16
        key = jax.random.key(seed)
        ks = jax.random.split(key, 12)
        B, L, D = (4, 256, 128)
        s = 1.0 / np.sqrt(D)
        return {'queries': jax.random.normal(ks[0], (B, L, D), dtype=jnp.float32), 'keys': jax.random.normal(ks[1], (B, L, D), dtype=jnp.float32), 'values': jax.random.normal(ks[2], (B, L, D), dtype=jnp.float32), 'Wq': jax.random.normal(ks[3], (D, D), dtype=jnp.float32) * s, 'bq': jnp.zeros((D,), dtype=jnp.float32), 'Wk': jax.random.normal(ks[4], (D, D), dtype=jnp.float32) * s, 'bk': jnp.zeros((D,), dtype=jnp.float32), 'Wv': jax.random.normal(ks[5], (D, D), dtype=jnp.float32) * s, 'bv': jnp.zeros((D,), dtype=jnp.float32), 'Wo': jax.random.normal(ks[6], (D, D), dtype=jnp.float32) * s, 'bo': jnp.zeros((D,), dtype=jnp.float32)}
    _L0_xattn_all = _L0_xattn_setup()
    _L0_xattn_in = {k: v for k, v in _L0_xattn_all.items() if k in ('Wq', 'bq', 'Wk', 'bk', 'Wv', 'bv', 'Wo', 'bo')}
    del _L0_xattn_all

    def _L0_ffn_setup():
        import jax, jax.numpy as jnp
        import numpy as np
        B, S, D_MODEL, D_HIDDEN = (4, 256, 128, 512)

        def act_quant(x):
            scale = 127.0 / jnp.clip(jnp.max(jnp.abs(x), axis=-1, keepdims=True), 1e-05)
            return jnp.clip(jnp.round(x * scale), -128, 127) / scale

        def weight_quant(w):
            scale = 1.0 / jnp.clip(jnp.mean(jnp.abs(w)), 1e-05)
            return jnp.clip(jnp.round(w * scale), -1, 1) / scale

        def bit_linear(x, w):
            xq = x + jax.lax.stop_gradient(act_quant(x) - x)
            wq = w + jax.lax.stop_gradient(weight_quant(w) - w)
            return jnp.einsum('bsd,hd->bsh', xq, wq)

        def depthwise_conv1d(x_bcl, w, b):
            y = jax.lax.conv_general_dilated(x_bcl, w, window_strides=(1,), padding=[(1, 1)], dimension_numbers=('NCH', 'OIH', 'NCH'), feature_group_count=x_bcl.shape[1])
            return y + b[None, :, None]
        key = jax.random.key(seed)
        ks = jax.random.split(key, 5)
        lim1 = 1.0 / np.sqrt(D_MODEL)
        lim2 = 1.0 / np.sqrt(D_HIDDEN)
        limc = 1.0 / np.sqrt(3.0)
        return {'x': jax.random.normal(ks[0], (B, S, D_MODEL), dtype=jnp.float32), 'w1': jax.random.uniform(ks[1], (D_HIDDEN, D_MODEL), jnp.float32, -lim1, lim1), 'conv_w': jax.random.uniform(ks[2], (D_HIDDEN, 1, 3), jnp.float32, -limc, limc), 'conv_b': jax.random.uniform(ks[3], (D_HIDDEN,), jnp.float32, -limc, limc), 'w2': jax.random.uniform(ks[4], (D_MODEL, D_HIDDEN), jnp.float32, -lim2, lim2)}
    _L0_ffn_all = _L0_ffn_setup()
    _L0_ffn_in = {k: v for k, v in _L0_ffn_all.items() if k in ('w1', 'conv_w', 'conv_b', 'w2')}
    del _L0_ffn_all
    return {'x': x, 'ctx_1024': ctx_1024, 'L0_xattn_Wq': _L0_xattn_in['Wq'], 'L0_xattn_bq': _L0_xattn_in['bq'], 'L0_xattn_Wk': _L0_xattn_in['Wk'], 'L0_xattn_bk': _L0_xattn_in['bk'], 'L0_xattn_Wv': _L0_xattn_in['Wv'], 'L0_xattn_bv': _L0_xattn_in['bv'], 'L0_xattn_Wo': _L0_xattn_in['Wo'], 'L0_xattn_bo': _L0_xattn_in['bo'], 'L0_ffn_w1': _L0_ffn_in['w1'], 'L0_ffn_conv_w': _L0_ffn_in['conv_w'], 'L0_ffn_conv_b': _L0_ffn_in['conv_b'], 'L0_ffn_w2': _L0_ffn_in['w2']}

def reference(x, ctx_1024, L0_xattn_Wq, L0_xattn_bq, L0_xattn_Wk, L0_xattn_bk, L0_xattn_Wv, L0_xattn_bv, L0_xattn_Wo, L0_xattn_bo, L0_ffn_w1, L0_ffn_conv_w, L0_ffn_conv_b, L0_ffn_w2):
    import jax
    import jax.numpy as jnp

    def _L0_xattn_ref(queries, keys, values, Wq, bq, Wk, bk, Wv, bv, Wo, bo):
        import jax, jax.numpy as jnp
        import numpy as np
        N_HEADS = 16
        B, L, D = queries.shape
        H = N_HEADS
        dk = D // H

        def split_heads(x):
            return x.reshape(B, L, H, dk).transpose(0, 2, 1, 3)
        q = split_heads(queries @ Wq + bq)
        k = split_heads(keys @ Wk + bk)
        v = split_heads(values @ Wv + bv)
        U = max(1, L // 2)
        q_norm = jnp.linalg.norm(q, axis=-1)
        _, idx = jax.lax.top_k(q_norm, U)
        idx_e = idx[..., None]
        q_s = jnp.take_along_axis(q, idx_e, axis=2)
        k_s = jnp.take_along_axis(k, idx_e, axis=2)
        v_s = jnp.take_along_axis(v, idx_e, axis=2)
        scores = jnp.einsum('bhud,bhwd->bhuw', q_s, k_s) / jnp.sqrt(jnp.float32(dk))
        attn = jax.nn.softmax(scores, axis=-1)
        context = jnp.einsum('bhuw,bhwd->bhud', attn, v_s)
        b_ix = jnp.arange(B)[:, None, None]
        h_ix = jnp.arange(H)[None, :, None]
        full = jnp.zeros((B, H, L, dk), dtype=context.dtype)
        full = full.at[b_ix, h_ix, idx, :].set(context)
        out = full.transpose(0, 2, 1, 3).reshape(B, L, D)
        return out @ Wo + bo

    def _L0_ffn_ref(x, w1, conv_w, conv_b, w2):
        import jax, jax.numpy as jnp
        import numpy as np
        B, S, D_MODEL, D_HIDDEN = (4, 256, 128, 512)

        def act_quant(x):
            scale = 127.0 / jnp.clip(jnp.max(jnp.abs(x), axis=-1, keepdims=True), 1e-05)
            return jnp.clip(jnp.round(x * scale), -128, 127) / scale

        def weight_quant(w):
            scale = 1.0 / jnp.clip(jnp.mean(jnp.abs(w)), 1e-05)
            return jnp.clip(jnp.round(w * scale), -1, 1) / scale

        def bit_linear(x, w):
            xq = x + jax.lax.stop_gradient(act_quant(x) - x)
            wq = w + jax.lax.stop_gradient(weight_quant(w) - w)
            return jnp.einsum('bsd,hd->bsh', xq, wq)

        def depthwise_conv1d(x_bcl, w, b):
            y = jax.lax.conv_general_dilated(x_bcl, w, window_strides=(1,), padding=[(1, 1)], dimension_numbers=('NCH', 'OIH', 'NCH'), feature_group_count=x_bcl.shape[1])
            return y + b[None, :, None]
        h = bit_linear(x, w1)
        h = depthwise_conv1d(h.transpose(0, 2, 1), conv_w, conv_b)
        h = h.transpose(0, 2, 1)
        h = jax.nn.silu(h)
        return bit_linear(h, w2)
    x = x + _L0_xattn_ref(_layernorm(x, axis=-1), ctx_1024, ctx_1024, L0_xattn_Wq, L0_xattn_bq, L0_xattn_Wk, L0_xattn_bk, L0_xattn_Wv, L0_xattn_bv, L0_xattn_Wo, L0_xattn_bo)
    x = x + _L0_ffn_ref(_layernorm(x, axis=-1), L0_ffn_w1, L0_ffn_conv_w, L0_ffn_conv_b, L0_ffn_w2)
    return x

_drawn_inputs = setup_inputs


def setup_inputs(seed=0):
    import zlib

    import numpy as np

    out = dict(_drawn_inputs(seed))
    spreads = {'L0_xattn_bq': (0.0, 0.1),
     'L0_xattn_bk': (0.0, 0.1),
     'L0_xattn_bv': (0.0, 0.1),
     'L0_xattn_bo': (0.0, 0.1)}
    factors = {}
    for name, (base, spread) in spreads.items():
        noise = np.random.default_rng([zlib.crc32(name.encode()), seed]).standard_normal(out[name].shape)
        drawn = base * np.exp(spread * noise) if base else spread * noise
        out[name] = jnp.asarray(drawn.astype(out[name].dtype))
    for name, factor in factors.items():
        out[name] = (out[name] * factor).astype(out[name].dtype)
    return out
```

```python
from contextlib import ExitStack

import concourse.bass as bass
from concourse import mybir

F32 = mybir.dt.float32
BF16 = mybir.dt.bfloat16
ALU = mybir.AluOpType
ACT = mybir.ActivationFunctionType
AX = mybir.AxisListType

ROUND = 1.5 * 2.0 ** 23
MASKED = -1.0e30
SMALLEST = 1e-5
EPS = 1e-5


def xattn_ffn_kernel(nc, x, ctx_in, Wq, bq, Wk, bk, Wv, bv, Wo, bo, w1, conv_w, conv_b, w2, out):
    B, T, D = x.shape
    H, DK = 16, 8
    HID = w1.shape[0]
    CT = HID // 128
    TAPS = conv_w.shape[2]
    G = 4
    NG = B // G
    GT = G * T
    GH = G * H
    NSEL = T // 2
    HP = H // 2
    PARTS = 3
    NPROD = 48
    KS = NPROD + 1
    KT = NPROD + 3
    VW = DK + 1
    UNITS = 16
    NBUF = 3
    SRING, TRING, PRING = 3, 2, 3
    SCALE = float(DK) ** -0.5
    LOADS = 15

    scr_q = nc.dram_tensor("scr_q", (NG, PARTS, D, GT), BF16).ap()
    scr_k = nc.dram_tensor("scr_k", (NG, PARTS, D, GT), BF16).ap()
    scr_v = nc.dram_tensor("scr_v", (NG, 128, GH * VW), F32).ap()
    scr_m = nc.dram_tensor("scr_m", (NG, GH, T), BF16).ap()

    x_g = x.rearrange("(g b) t d -> g t b d", b=G)
    ctx_g = ctx_in.rearrange("(g b) t d -> g t b d", b=G)
    out_g = out.rearrange("(g b) t d -> g t b d", b=G)

    with ExitStack() as ctx:
        def sb(name, shape, dt):
            return ctx.enter_context(nc.sbuf_tensor(name, shape, dt))

        def sem(name):
            return ctx.enter_context(nc.semaphore(name))

        bank = [ctx.enter_context(nc.psum_tensor(f"bank{i}", [128, 512], F32)) for i in range(8)]

        ident = sb("ident", [128, 128], F32)
        ones = sb("ones", [128, 128], F32)
        minus_half = sb("minus_half", [128, G], F32)
        wq_sb = sb("wq_sb", [D, D], F32)
        wk_sb = sb("wk_sb", [D, D], F32)
        wqp = sb("wqp", [D, D], F32)
        wkp = sb("wkp", [D, D], F32)
        wv_sb = sb("wv_sb", [D, D], F32)
        wo_sb = sb("wo_sb", [D, D], F32)
        bq_c = sb("bq_c", [D, 1], F32)
        bk_c = sb("bk_c", [D, 1], F32)
        bv_r = sb("bv_r", [128, D], F32)
        bo_r = sb("bo_r", [128, D], F32)
        w1_n = sb("w1_n", [128, CT, D], F32)
        w2_n = sb("w2_n", [128, HID], F32)
        cw = sb("cw", [128, CT, TAPS], F32)
        cb = sb("cb", [128, CT], F32)
        wabs = sb("wabs", [128, 2], F32)
        wsc = sb("wsc", [128, 2], F32)
        winv = sb("winv", [128, 2], F32)
        wtmp = sb("wtmp", [128, 512], F32)
        wtap = sb("wtap", [128, CT, TAPS, D], F32)
        w2t = sb("w2t", [128, CT, D], BF16)
        w1t = sb("w1t", [D, CT, TAPS, 128], F32)
        x_all = sb("x_all", [128, B * D], F32)
        mask_all = sb("mask_all", [128, B * H], F32)

        ctx_sb = sb("ctx_sb", [128, GT], F32)
        stats = sb("stats", [128, G, 6], F32)
        mv = sb("mv", [128, G, 2], F32)
        vare = sb("vare", [128, G], F32)
        rstd = sb("rstd", [128, G], F32)
        xn = sb("xn", [128, GT], F32)
        xT = sb("xT", [128, GT], F32)
        cT = sb("cT", [128, GT], F32)
        q32 = sb("q32", [128, GT], F32)
        k32 = sb("k32", [128, GT], F32)
        qr = sb("qr", [128, GT], F32)
        kr = sb("kr", [128, GT], F32)
        qp = sb("qp", [128, PARTS, GT], BF16)
        kp = sb("kp", [128, PARTS, GT], BF16)
        vx = sb("vx", [128, GH, VW], F32)
        sq = sb("sq", [128, GT], F32)
        norm2 = sb("norm2", [128, GH], F32)
        work = sb("work", [GH, T], F32)
        top8 = sb("top8", [GH, NSEL // 8, 8], F32)
        maskT = sb("maskT", [GH, T], F32)
        negmask = sb("negmask", [GH, T], BF16)

        qop = [sb(f"qop{i}", [128, HP, GT], BF16) for i in range(NBUF)]
        kop = [sb(f"kop{i}", [128, HP, GT], BF16) for i in range(NBUF)]
        vop = [sb(f"vop{i}", [128, GH, VW], F32) for i in range(NBUF)]
        negmax = [sb(f"negmax{i}", [128, H], F32) for i in range(2)]
        nmT = [sb(f"nmT{i}", [H, 2, T], BF16) for i in range(2)]
        probs = [sb(f"probs{i}", [128, 512], F32) for i in range(PRING)]
        ctxU = sb("ctxU", [128, 512], F32)
        rden = sb("rden", [128, H], F32)
        rmask = sb("rmask", [128, H], F32)
        ctxn = sb("ctxn", [128, H, DK], F32)
        ctxT = sb("ctxT", [128, T], F32)

        xn2 = sb("xn2", [128, G, D], F32)
        xr = sb("xr", [128, G, D], F32)
        amax = sb("amax", [128, G], F32)
        amaxc = sb("amaxc", [128, G], F32)
        arec = sb("arec", [128, G], F32)
        asc = sb("asc", [128, G], F32)
        ainv = sb("ainv", [128, G], F32)
        xqT = sb("xqT", [128, G, T + 2], F32)
        z = sb("z", [128, CT, GT], F32)
        zs = sb("zs", [128, CT, GT], F32)
        zi = sb("zi", [128, CT, GT], BF16)
        zmax = sb("zmax", [128, G], F32)
        zmaxc = sb("zmaxc", [128, G], F32)
        zrec = sb("zrec", [128, G], F32)
        zsc = sb("zsc", [128, G], F32)
        zinv = sb("zinv", [128, G], F32)
        zout = sb("zout", [128, G], F32)
        diag = sb("diag", [128, G, 128], F32)
        scb = sb("scb", [128, GT], F32)
        osb = sb("osb", [128, GT], F32)

        names = """ops_free spare wp_ok const_p w_in w2_in const_z const_i const_v w_step wabs_ps wtr_ps w_sb
            x_in ctx_in_s st_q st_k st_v st_m
            stat_step var_ok rstd_ok xn_ok xT_ps cT_ps xT_sb cT_sb q_ps k_ps v_ps q32_ok qhi_ok k32_ok khi_ok
            n_ps sq_ok norm_ok nT_ps work_ok top_step maskT_ok negm_ok m_ps mask_ok v_sb
            qr_ok kr_ok qmid_ok kmid_ok qlo_ok klo_ok xbo_ok
            s_done max_ok t_done exp_ok pv_unit pv_b cU_ok nat_ps att_step ctxn_ok cT2_ps cT2_sb proj_ps x1_ok
            nm_ps nm_hi nm_ok
            stat3 var3 rstd3 f_step xq_ok xqT_ps xqT_sb y_ps z_ok zt_ps zmax_ok diag_ok sc_ps scb_ok
            zs_ok zi_ok o_ps o_ok out_st""".split()
        S = {n: sem(n) for n in names}
        op_in = [sem(f"op_in{i}") for i in range(NBUF)]
        nm_in = [sem(f"nm_in{i}") for i in range(G)]

        def apart(eng, s, n):
            eng.wait_ge(s, n)
            eng.sem_inc(S["spare"], 1)

        def grp(t, g):
            return t[:, bass.ds(g * GT, GT)]

        block = ctx.enter_context(nc.Block())
        psX, psC, psQ, psK, psV, psN, psM, psW = bank
        sbank, tbank, pvbank, natbank, mbank = bank[0:3], bank[3:5], bank[5], bank[6], bank[7]
        ybank, ztbank, scbank, obank, xqbank = bank[0:2], bank[2:4], bank[4], bank[5], bank[6]

        @block.sync
        def _(sp):
            def load_x(g):
                sp.dma_start(grp(x_all, g).rearrange("p (b d) -> p b d", b=G), x_g[g]).then_inc(S["x_in"], 16)

            def load_ctx(g):
                sp.dma_start(ctx_sb[:, :].rearrange("p (b d) -> p b d", b=G), ctx_g[g]).then_inc(S["ctx_in_s"], 16)

            load_x(0)
            load_ctx(0)
            for dst, src in ((wq_sb, Wq), (wk_sb, Wk), (wv_sb, Wv), (wo_sb, Wo)):
                sp.dma_start(dst[:, :], src).then_inc(S["w_in"], 16)
            for dst, src in ((bq_c, bq), (bk_c, bk)):
                for h in range(2):
                    sp.dma_start(dst[64 * h:64 * h + 64, :],
                                 src.rearrange("(h k d a) -> h d k a", h=2, d=DK, a=1)[h],
                                 allow_slow_non_contiguous=True).then_inc(S["w_in"], 16)
            sp.dma_start(bv_r[:, :], bv.partition_broadcast(128)).then_inc(S["w_in"], 16)
            sp.dma_start(bo_r[:, :], bo.partition_broadcast(128)).then_inc(S["w_in"], 16)
            sp.dma_start(w1_n[:, :, :], w1.rearrange("(c p) d -> p c d", p=128)).then_inc(S["w2_in"], 16)
            sp.dma_start(w2_n[:, :], w2).then_inc(S["w2_in"], 16)
            sp.dma_start(cw[:, :, :], conv_w.rearrange("(c p) a k -> p c (a k)", p=128)).then_inc(S["w2_in"], 16)
            for c in range(CT):
                sp.dma_start(cb[:, c:c + 1], conv_b[c * 128:(c + 1) * 128].rearrange("(p a) -> p a", a=1))\
                    .then_inc(S["w2_in"], 16)

            def store(g):
                sp.wait_ge(S["qlo_ok"], g + 1)
                sp.wait_ge(S["qmid_ok"], g + 1)
                sp.wait_ge(S["qhi_ok"], g + 1)
                sp.dma_start(scr_q[g].rearrange("a p t -> p a t"), qp[:, :, :]).then_inc(S["st_q"], 16)
                sp.wait_ge(S["klo_ok"], g + 1)
                sp.wait_ge(S["kmid_ok"], g + 1)
                sp.wait_ge(S["khi_ok"], g + 1)
                sp.dma_start(scr_k[g].rearrange("a p t -> p a t"), kp[:, :, :]).then_inc(S["st_k"], 16)
                sp.wait_ge(S["v_sb"], g + 1)
                sp.dma_start(scr_v[g], vx[:, :, :].rearrange("p h c -> p (h c)")).then_inc(S["st_v"], 16)
                sp.wait_ge(S["negm_ok"], g + 1)
                sp.dma_start(scr_m[g], negmask[:, :]).then_inc(S["st_m"], 16)

            def stage1(g):
                sp.wait_ge(S["x_in"], g * 16)
                load_x(g)
                sp.wait_ge(S["ctx_in_s"], g * 16)
                sp.wait_ge(S["cT_ps"], g)
                load_ctx(g)

            stage1(1)
            store(0)
            with sp.Fori(2, NG) as g:
                stage1(g)
                store(g - 1)
            store(NG - 1)

            def load_ops(g, buf):
                for s in ("st_q", "st_k", "st_v", "st_m"):
                    sp.wait_ge(S[s], 16 * (g + 1))
                inc = op_in[buf]
                for half in range(2):
                    p0 = 64 * half
                    for dst, scr, is_k in ((qop[buf], scr_q, False), (kop[buf], scr_k, True)):
                        src = scr[g].rearrange("a (h d k) t -> h d a (k t)", h=2, d=DK)[half]
                        row = p0
                        for qpart, n in ((0, 3), (1, 2), (2, 1)):
                            if is_k:
                                s = src[:, 0:n]
                            else:
                                s = src[:, qpart:qpart + 1].broadcast_to([DK, n, HP * GT]) if n > 1 else src[:, qpart:qpart + 1]
                            sp.dma_start(dst[row:row + DK * n, :, :].rearrange("p k t -> p (k t)"), s).then_inc(inc, 16)
                            row += DK * n
                    sp.dma_start(kop[buf][p0 + NPROD:p0 + NPROD + 1, :, :].rearrange("p k (b t) -> p k b t", b=G),
                                 scr_m[g].rearrange("(b h k) t -> h k b t", b=G, h=2)[half:half + 1]).then_inc(inc, 16)
                sp.dma_start(vop[buf][:, :, :].rearrange("p h c -> p (h c)"), scr_v[g]).then_inc(inc, 16)

            def move_max(s, b, buf):
                sp.wait_ge(S["nm_ok"], 4 * s + b + 1)
                for half in range(2):
                    for part in range(2):
                        row = 64 * half + KS + part
                        sp.dma_start(qop[buf][row:row + 1, :, b * T:(b + 1) * T],
                                     nmT[b % 2][HP * half:HP * half + HP, part, :]).then_inc(nm_in[b], 16)

            sp.wait_ge(S["const_p"], 2 * NBUF)
            load_ops(0, 0)
            load_ops(1, 1)
            for b in range(3):
                move_max(0, b, 0)
            sp.sem_inc(S["ops_free"], 1)
            with sp.Fori(0, 2) as r:
                for j in range(NBUF):
                    s = 3 * r + 2 + j
                    sp.wait_ge(S["ops_free"], s - 1)
                    load_ops(s, (2 + j) % NBUF)
                    move_max(s - 2, 3, j % NBUF)
                    for b in range(3):
                        move_max(s - 1, b, (1 + j) % NBUF)
            move_max(6, 3, 0)
            for b in range(4):
                move_max(7, b, 1)

            def store_out(g):
                sp.wait_ge(S["o_ok"], g + 1)
                sp.dma_start(out_g[g], osb[:, :].rearrange("p (b d) -> p b d", b=G)).then_inc(S["out_st"], 16)
            with sp.Fori(0, NG) as g:
                store_out(g)
            sp.wait_ge(S["out_st"], 16 * NG)

        @block.gpsimd
        def _(pool):
            pool.memset(ident[:, :], 0.0).then_inc(S["const_z"], 1)
            pool.wait_ge(S["const_z"], 1)
            pool.affine_select(out=ident[:, :], in_=ident[:, :], compare_op=ALU.not_equal, fill=1.0, base=0,
                               pattern=[[-1, 128]], channel_multiplier=1).then_inc(S["const_i"], 1)
            pool.memset(minus_half[:, :], -0.5).then_inc(S["const_z"], 1)
            pool.wait_ge(S["const_z"], 2)
            pool.wait_ge(S["w_in"], 16 * 10)

            def inv_std(ok_in, ok_out, n):
                pool.wait_ge(ok_in, n)
                pool.tensor_tensor(rstd[:, :], vare[:, :], minus_half[:, :], ALU.pow).then_inc(ok_out, 1)

            def split(g):
                for f, part, r, t in (("q", qp, qr, q32), ("k", kp, kr, k32)):
                    pool.wait_ge(S[f + "hi_ok"], g + 1)
                    pool.wait_ge(S[f + "32_ok"], g + 1)
                    if not (isinstance(g, int) and g < 1):
                        pool.wait_ge(S[f + "lo_ok"], g)
                    pool.tensor_tensor(r[:, :], t[:, :], part[:, 0, :], ALU.subtract).then_inc(S[f + "r_ok"], 1)
                for f, part, r in (("q", qp, qr), ("k", kp, kr)):
                    pool.wait_ge(S[f + "mid_ok"], g + 1)
                    pool.tensor_tensor(part[:, 2, :], r[:, :], part[:, 1, :], ALU.subtract).then_inc(S[f + "lo_ok"], 1)

            def add_bo(g):
                pool.wait_ge(S["xn_ok"], g + 1)
                xg = grp(x_all, g).rearrange("p (b d) -> p b d", b=G)
                pool.tensor_tensor(xg, xg, bo_r[:, :].unsqueeze(1).broadcast_to([128, G, D]), ALU.add).then_inc(S["xbo_ok"], 1)

            inv_std(S["var_ok"], S["rstd_ok"], 1)
            add_bo(0)
            split(0)
            inv_std(S["var_ok"], S["rstd_ok"], 2)
            for t in qop + kop:
                pool.memset(t[:, :, :], 1.0).then_inc(S["const_p"], 1)
            with pool.Fori(1, NG - 1) as g:
                add_bo(g)
                split(g)
                inv_std(S["var_ok"], S["rstd_ok"], g + 2)
            add_bo(NG - 1)
            split(NG - 1)

            def stage3(g):
                inv_std(S["var3"], S["rstd3"], g + 1)
                pool.wait_ge(S["scb_ok"], g + 1)
                pool.wait_ge(S["z_ok"], CT * (g + 1))
                for c in range(CT):
                    pool.tensor_tensor(zs[:, c, :], z[:, c, :], scb[:, :], ALU.mult).then_inc(S["zs_ok"], 1)

            stage3(0)
            with pool.Fori(1, NG) as g:
                pool.wait_ge(S["zi_ok"], g)
                stage3(g)

        @block.scalar
        def _(act):
            act.wait_ge(S["w_in"], 16 * 10)

            def parts(g, f, ps, t32, part, bias):
                act.wait_ge(S[f + "_ps"], g + 1)
                if not (isinstance(g, int) and g < 1):
                    act.wait_ge(S[f + "lo_ok"], g)
                    act.wait_ge(S["n_ps"], g)
                    act.wait_ge(S["st_" + f], 16 * g)
                act.activation(t32[:, :], ps[:, :], ACT.Identity, bias=bias[:, 0:1]).then_inc(S[f + "32_ok"], 1)
                act.activation(part[:, 0, :], ps[:, :], ACT.Identity, bias=bias[:, 0:1]).then_inc(S[f + "hi_ok"], 1)

            def stage1(g):
                act.wait_ge(S["xT_ps"], g + 1)
                act.activation(xT[:, :], psX[:, :], ACT.Copy).then_inc(S["xT_sb"], 1)
                act.wait_ge(S["cT_ps"], g + 1)
                if not (isinstance(g, int) and g < 1):
                    act.wait_ge(S["v_ps"], g)
                act.activation(cT[:, :], psC[:, :], ACT.Copy).then_inc(S["cT_sb"], 1)
                parts(g, "q", psQ, q32, qp, bq_c)
                parts(g, "k", psK, k32, kp, bk_c)
                act.wait_ge(S["n_ps"], g + 1)
                if not (isinstance(g, int) and g < 1):
                    act.wait_ge(S["norm_ok"], g)
                act.activation(sq[:, :], psN[:, :], ACT.Square).then_inc(S["sq_ok"], 1)
                for f, part, r in (("q", qp, qr), ("k", kp, kr)):
                    act.wait_ge(S[f + "r_ok"], g + 1)
                    act.activation(part[:, 1, :], r[:, :], ACT.Copy).then_inc(S[f + "mid_ok"], 1)

            stage1(0)
            with act.Fori(1, NG) as g:
                stage1(g)

            def attend(t, j):
                first = isinstance(t, int) and t == 0
                for n in range(UNITS):
                    N = UNITS * t + n
                    act.wait_ge(S["t_done"], N + 1)
                    if not (first and n < PRING):
                        act.wait_ge(S["pv_unit"], N - PRING + 1)
                    act.activation(probs[(UNITS * j + n) % PRING][:, :], tbank[n % TRING][:, :], ACT.Exp,
                                   scale=SCALE).then_inc(S["exp_ok"], 1)
                    beta = 4 * t + n // 4 - 1
                    if not (first and n < 4):
                        if n % 4 == 1:
                            context(beta)
                        if n == 1:
                            act.sem_inc(S["ops_free"], 1)
                        if n % 4 == 3:
                            turned(beta)

            def context(beta):
                act.wait_ge(S["pv_unit"], 4 * (beta + 1))
                act.wait_ge(S["nat_ps"], beta)
                act.activation(ctxU[:, :], pvbank[:, :], ACT.Copy).then_inc(S["cU_ok"], 1)

            def turned(beta):
                act.wait_ge(S["cT2_ps"], beta + 1)
                act.wait_ge(S["proj_ps"], beta)
                act.activation(ctxT[:, :], mbank[:, 0:T], ACT.Copy).then_inc(S["cT2_sb"], 1)

            attend(0, 0)
            with act.Fori(0, 2) as r:
                for j in range(3):
                    attend(3 * r + 1 + j, (1 + j) % NBUF)
            attend(7, 1)
            context(4 * NG - 1)
            turned(4 * NG - 1)

            def stage3(g):
                act.wait_ge(S["xqT_ps"], g + 1)
                if not (isinstance(g, int) and g < 1):
                    act.wait_ge(S["y_ps"], CT * g)
                act.activation(xqT[:, :, 1:T + 1], xqbank[:, :].rearrange("p (b t) -> p b t", b=G),
                               ACT.Copy).then_inc(S["xqT_sb"], 1)
                for c in range(CT):
                    act.wait_ge(S["y_ps"], CT * g + c + 1)
                    if not (isinstance(g, int) and g < 1):
                        if c == 0:
                            act.wait_ge(S["zs_ok"], CT * g)
                            act.wait_ge(S["zt_ps"], G * g)
                    act.activation(z[:, c, :], ybank[c % 2][:, :], ACT.Silu, bias=cb[:, c:c + 1]).then_inc(S["z_ok"], 1)
                act.wait_ge(S["sc_ps"], g + 1)
                act.activation(scb[:, :], scbank[:, :], ACT.Copy).then_inc(S["scb_ok"], 1)

            act.wait_ge(S["w2_in"], 16 * (3 + CT))
            stage3(0)
            with act.Fori(1, NG) as g:
                stage3(g)

        @block.vector
        def _(dve):
            dve.memset(ones[:, :], 1.0).then_inc(S["const_v"], 1)
            dve.memset(vx[:, :, :], 1.0).then_inc(S["const_v"], 1)
            dve.memset(xqT[:, :, :], 0.0).then_inc(S["const_v"], 1)

            def stats_of(g, step, ok, count):
                for b in range(G):
                    dve.bn_stats(stats[:, b, :], x_all[:, bass.ds(g * GT + b * D, D)]).then_inc(step, 1)
                apart(dve, step, count * 2 * G + G)
                for b in range(G):
                    dve.bn_aggr(mv[:, b, :], stats[:, b, :]).then_inc(step, 1)
                dve.wait_ge(step, (count + 1) * 2 * G)
                dve.tensor_scalar(vare[:, :], mv[:, :, 1], EPS, None, ALU.add).then_inc(ok, 1)

            def normalise(g, dst):
                for b in range(G):
                    last = dve.tensor_scalar(dst[:, b * D:(b + 1) * D], x_all[:, bass.ds(g * GT + b * D, D)],
                                             mv[:, b, 0:1], rstd[:, b:b + 1], ALU.subtract, ALU.mult)
                return last

            def select(g):
                dve.wait_ge(S["nT_ps"], g + 1)
                dve.tensor_copy(work[:, :], psM[0:GH, 0:T]).then_inc(S["top_step"], 1)
                n = 2 * (NSEL // 8) + 1
                for i in range(NSEL // 8):
                    apart(dve, S["top_step"], n * g + 2 * i + 1)
                    dve.max(top8[:, i, :], work[:, :]).then_inc(S["top_step"], 1)
                    apart(dve, S["top_step"], n * g + 2 * i + 2)
                    dve.match_replace(work[:, :], top8[:, i, :], work[:, :], -1.0).then_inc(S["top_step"], 1)
                dve.wait_ge(S["top_step"], n * (g + 1))
                if not (isinstance(g, int) and g < 1):
                    dve.wait_ge(S["st_m"], 16 * g)
                dve.tensor_scalar(negmask[:, :], work[:, :], 0.0, MASKED, ALU.is_ge, ALU.mult).then_inc(S["negm_ok"], 1)
                dve.tensor_scalar(maskT[:, :], work[:, :], 0.0, None, ALU.is_lt).then_inc(S["maskT_ok"], 1)

            def keep_mask(g):
                dve.wait_ge(S["m_ps"], g + 1)
                dve.tensor_copy(mask_all[:, bass.ds(g * GH, GH)], psM[:, T:T + GH]).then_inc(S["mask_ok"], 1)

            def stage1(g, more):
                first = isinstance(g, int) and g < 1
                dve.wait_ge(S["rstd_ok"], g + 1)
                if not first:
                    dve.wait_ge(S["xT_ps"], g)
                normalise(g, xn).then_inc(S["xn_ok"], 1)
                dve.wait_ge(S["v_ps"], g + 1)
                if not first:
                    dve.wait_ge(S["st_v"], 16 * g)
                dve.tensor_tensor(vx[:, :, 0:DK].rearrange("p (b h) c -> p b h c", b=G),
                                  psV[:, :].rearrange("p (b h c) -> p b h c", b=G, c=DK),
                                  bv_r[:, :].rearrange("p (h c) -> p h c", c=DK).unsqueeze(1).broadcast_to([128, G, H, DK]),
                                  ALU.add).then_inc(S["v_sb"], 1)
                if not first:
                    select(g - 1)
                dve.wait_ge(S["sq_ok"], g + 1)
                dve.tensor_reduce(norm2[:, :], sq[:, :].rearrange("p (h d k) -> p h k d", d=DK, k=HP), AX.X, ALU.add).then_inc(S["norm_ok"], 1)
                if not first:
                    keep_mask(g - 1)
                if more:
                    dve.wait_ge(S["x_in"], 16 * (g + 2))
                    dve.wait_ge(S["xn_ok"], g + 1)
                    stats_of(g + 1, S["stat_step"], S["var_ok"], g + 1)

            dve.wait_ge(S["const_v"], 3)
            dve.wait_ge(S["x_in"], 16)
            stats_of(0, S["stat_step"], S["var_ok"], 0)
            dve.wait_ge(S["w_in"], 16 * 10)
            for dst, src in ((wqp, wq_sb), (wkp, wk_sb)):
                for h in range(2):
                    dve.tensor_copy(dst[:, 64 * h:64 * h + 64].rearrange("p (d k) -> p d k", d=DK),
                                    src[:, 64 * h:64 * h + 64].rearrange("p (k d) -> p d k", d=DK)).then_inc(S["wp_ok"], 1)
            stage1(0, True)

            wstep = [0]

            def chain(ins):
                wstep[0] += 1
                ins.then_inc(S["w_step"], 1)
                dve.wait_ge(S["w_step"], wstep[0])

            dve.wait_ge(S["w2_in"], 16 * (3 + CT))
            chain(dve.tensor_reduce(wabs[:, 0:1], w1_n[:, :, :], AX.XY, ALU.add, apply_absolute_value=True))
            chain(dve.tensor_reduce(wabs[:, 1:2], w2_n[:, :], AX.X, ALU.add, apply_absolute_value=True))
            dve.wait_ge(S["wabs_ps"], 1)
            chain(dve.tensor_scalar(wabs[:, :], psW[:, 0:2], 1.0 / (HID * D), SMALLEST, ALU.mult, ALU.max))
            chain(dve.reciprocal(wsc[:, :], wabs[:, :]))
            chain(dve.reciprocal(winv[:, :], wsc[:, :]))
            w1f = w1_n[:, :, :].rearrange("p c d -> p (c d)")
            for wf, k in ((w1f, 0), (w2_n[:, :], 1)):
                chain(dve.tensor_scalar(wtmp[:, :], wf, wsc[:, k:k + 1], ROUND, ALU.mult, ALU.add))
                chain(dve.tensor_scalar(wtmp[:, :], wtmp[:, :], ROUND, 1.0, ALU.subtract, ALU.min))
                chain(dve.tensor_scalar(wf, wtmp[:, :], -1.0, None, ALU.max))
            chain(dve.tensor_scalar(w1f, w1f, winv[:, 0:1], None, ALU.mult))
            for c in range(CT):
                for k in range(TAPS):
                    chain(dve.tensor_scalar(wtap[:, c, k, :], w1_n[:, c, :], cw[:, c, k:k + 1], None, ALU.mult))
            for i in range(4):
                dve.wait_ge(S["wtr_ps"], i + 1)
                if i < 3:
                    dve.tensor_copy(w1t[:, :, i, :], psW[:, :].rearrange("p (c k) -> p c k", c=CT)).then_inc(S["w_sb"], 1)
                else:
                    dve.tensor_copy(w2t[:, :, :], psW[:, :].rearrange("p (c k) -> p c k", c=CT)).then_inc(S["w_sb"], 1)

            with dve.Fori(1, NG - 1) as g:
                stage1(g, True)
            stage1(NG - 1, False)
            select(NG - 1)
            keep_mask(NG - 1)

            def maximum(s, j, n):
                N = UNITS * s + n
                dve.wait_ge(S["s_done"], N + 1)
                b, half, q4 = n // 4, n % 2, n % 4 // 2
                if n % 4 == 0 and not (isinstance(s, int) and s == 0 and n < 8):
                    dve.wait_ge(S["nm_ps"], 4 * s + b - 1)
                h0 = HP * half + 4 * q4
                dve.tensor_reduce(negmax[b % 2][:, h0:h0 + 4],
                                  sbank[(UNITS * j + n) % SRING][:, :].rearrange("p (h k) -> p h k", h=4),
                                  AX.X, ALU.max, negate=True).then_inc(S["max_ok"], 1)

            def split_max(sb_index, b):
                dve.wait_ge(S["nm_ps"], sb_index + 1)
                if b >= 2:
                    pass
                dve.tensor_copy(nmT[b % 2][:, 0, :], mbank[0:H, 0:T]).then_inc(S["nm_hi"], 1)
                dve.wait_ge(S["nm_hi"], sb_index + 1)
                dve.tensor_tensor(nmT[b % 2][:, 1, :], mbank[0:H, 0:T], nmT[b % 2][:, 0, :],
                                  ALU.subtract).then_inc(S["nm_ok"], 1)

            def weigh(beta):
                dve.wait_ge(S["nat_ps"], beta + 1)
                nat = natbank[:, :].rearrange("p (h r) -> p h r", r=32)
                dve.reciprocal(rden[:, :], nat[:, :, DK]).then_inc(S["att_step"], 1)
                dve.wait_ge(S["att_step"], 2 * beta + 1)
                dve.tensor_tensor(rmask[:, :], rden[:, :], mask_all[:, bass.ds(beta * H, H)], ALU.mult)\
                    .then_inc(S["att_step"], 1)
                dve.wait_ge(S["att_step"], 2 * beta + 2)
                dve.wait_ge(S["cT2_ps"], beta)
                dve.tensor_tensor(ctxn[:, :, :], nat[:, :, 0:DK], rmask[:, :].unsqueeze(2).broadcast_to([128, H, DK]),
                                  ALU.mult).then_inc(S["ctxn_ok"], 1)

            def residual(beta):
                dve.wait_ge(S["proj_ps"], beta + 1)
                xb = x_all[:, bass.ds(beta * D, D)]
                dve.tensor_tensor(xb, mbank[:, 0:D], xb, ALU.add).then_inc(S["x1_ok"], 1)

            def attend(s, sj, t):
                for n in range(UNITS):
                    if s is not None:
                        maximum(s, sj, n)
                    if n % 4 == 0:
                        if t is not None and not (isinstance(t, int) and t == 0 and n < 8):
                            residual(4 * t + n // 4 - 2)
                    if n % 4 == 2:
                        sbatch = (4 * s if s is not None else 4 * NG) + n // 4 - 1
                        b = (n // 4 - 1) % 4
                        if (s is not None or n == 2) and not (isinstance(s, int) and s == 0 and n < 4):
                            if not (isinstance(s, int) and (s == 0 and b < 2)):
                                prev = (b - 2) % 4
                                rounds = (s if s is not None else NG) - (1 if n < 4 else 0) - (1 if b < 2 else 0)
                                if not (isinstance(rounds, int) and rounds < 0):
                                    dve.wait_ge(nm_in[prev], 64 * (rounds + 1))
                            split_max(sbatch, b)
                        if t is not None and not (isinstance(t, int) and t == 0 and n < 4):
                            weigh(4 * t + n // 4 - 1)

            dve.memset(pvbank[:, :], 0.0).then_inc(S["const_v"], 1)
            dve.wait_ge(S["xbo_ok"], NG)
            attend(0, 0, None)
            attend(1, 1, 0)
            with dve.Fori(0, 2) as r:
                for j in range(3):
                    attend(3 * r + 2 + j, (2 + j) % NBUF, 3 * r + 1 + j)
            attend(None, None, 7)
            residual(4 * NG - 2)
            weigh(4 * NG - 1)
            residual(4 * NG - 1)

            def stage3(g):
                first = isinstance(g, int) and g < 1
                nf = 9 + 2 * G

                def f(k):
                    dve.wait_ge(S["f_step"], nf * g + k)

                if not first:
                    pass
                stats_of(g, S["stat3"], S["var3"], g)
                dve.wait_ge(S["rstd3"], g + 1)
                normalise(g, xn2[:, :, :].rearrange("p b d -> p (b d)")).then_inc(S["f_step"], 1)
                f(1)
                dve.tensor_reduce(amax[:, :], xn2[:, :, :], AX.X, ALU.max, apply_absolute_value=True).then_inc(S["f_step"], 1)
                f(2)
                dve.tensor_scalar(amaxc[:, :], amax[:, :], SMALLEST, None, ALU.max).then_inc(S["f_step"], 1)
                f(3)
                dve.reciprocal(arec[:, :], amaxc[:, :]).then_inc(S["f_step"], 1)
                f(4)
                dve.tensor_scalar(asc[:, :], arec[:, :], 127.0, None, ALU.mult).then_inc(S["f_step"], 1)
                f(5)
                dve.reciprocal(ainv[:, :], asc[:, :]).then_inc(S["f_step"], 1)
                for b in range(G):
                    dve.tensor_scalar(xr[:, b, :], xn2[:, b, :], asc[:, b:b + 1], ROUND, ALU.mult, ALU.add)\
                        .then_inc(S["f_step"], 1)
                f(6 + G)
                if not first:
                    dve.wait_ge(S["xqT_ps"], g)
                for b in range(G):
                    last = dve.tensor_scalar(xn[:, b * D:(b + 1) * D], xr[:, b, :], ROUND, ainv[:, b:b + 1],
                                             ALU.subtract, ALU.mult)
                last.then_inc(S["xq_ok"], 1)
                for b in range(G):
                    dve.wait_ge(S["zt_ps"], G * g + b + 1)
                    dve.tensor_reduce(zmax[:, b:b + 1], ztbank[b % 2][:, :], AX.X, ALU.max, apply_absolute_value=True)\
                        .then_inc(S["zmax_ok"], 1)
                dve.wait_ge(S["zmax_ok"], G * (g + 1))
                dve.tensor_scalar(zmaxc[:, :], zmax[:, :], SMALLEST, None, ALU.max).then_inc(S["f_step"], 1)
                f(7 + G)
                dve.reciprocal(zrec[:, :], zmaxc[:, :]).then_inc(S["f_step"], 1)
                f(8 + G)
                dve.tensor_scalar(zsc[:, :], zrec[:, :], 127.0, None, ALU.mult).then_inc(S["f_step"], 1)
                f(9 + G)
                for b in range(G):
                    last = dve.tensor_scalar(diag[:, b, :], ident[:, :], zsc[:, b:b + 1], None, ALU.mult)
                    last.then_inc(S["f_step"], 1)
                f(nf)
                dve.reciprocal(zinv[:, :], zsc[:, :]).then_inc(S["diag_ok"], 1)
                dve.wait_ge(S["diag_ok"], 2 * g + 1)
                dve.tensor_scalar(zout[:, :], zinv[:, :], winv[:, 1:2], None, ALU.mult).then_inc(S["diag_ok"], 1)
                if not first:
                    dve.wait_ge(S["o_ps"], g)
                for c in range(CT):
                    dve.wait_ge(S["zs_ok"], CT * g + c + 1)
                    last = dve.tensor_scalar(zi[:, c, :], zs[:, c, :], ROUND, ROUND, ALU.add, ALU.subtract)
                last.then_inc(S["zi_ok"], 1)
                dve.wait_ge(S["o_ps"], g + 1)
                if not first:
                    dve.wait_ge(S["out_st"], 16 * g)
                for b in range(G):
                    last = dve.scalar_tensor_tensor(out=osb[:, b * D:(b + 1) * D], in0=obank[:, b * D:(b + 1) * D],
                                                    scalar=zout[:, b:b + 1], in1=x_all[:, bass.ds(g * GT + b * D, D)],
                                                    op0=ALU.mult, op1=ALU.add)
                last.then_inc(S["o_ok"], 1)

            dve.wait_ge(S["x1_ok"], B)
            stage3(0)
            with dve.Fori(1, NG) as g:
                stage3(g)

        @block.tensor
        def _(pe):
            pe.wait_ge(S["const_i"], 1)
            pe.wait_ge(S["const_v"], 3)
            pe.wait_ge(S["w_in"], 16 * 10)

            def four(dst, src):
                for b in range(4):
                    last = pe.transpose(dst[:, b * 128:(b + 1) * 128], src(b), ident[:, :])
                return last

            def norms(g):
                if not (isinstance(g, int) and g < 1):
                    pe.wait_ge(S["mask_ok"], g)
                apart(pe, S["norm_ok"], g + 1)
                pe.transpose(psM[0:GH, 0:T], norm2[:, :], ident[:, :]).then_inc(S["nT_ps"], 1)

            def masks(g):
                apart(pe, S["maskT_ok"], g + 1)
                pe.transpose(psM[:, T:T + GH], maskT[:, :], ident[0:GH, 0:GH]).then_inc(S["m_ps"], 1)

            def stage1(g):
                first = isinstance(g, int) and g < 1
                if not first:
                    norms(g - 1)
                pe.wait_ge(S["xn_ok"], g + 1)
                four(psX, lambda b: xn[:, b * 128:(b + 1) * 128]).then_inc(S["xT_ps"], 1)
                pe.wait_ge(S["ctx_in_s"], 16 * (g + 1))
                four(psC, lambda b: ctx_sb[:, b * 128:(b + 1) * 128]).then_inc(S["cT_ps"], 1)
                pe.wait_ge(S["xT_sb"], g + 1)
                if not first:
                    pe.wait_ge(S["qhi_ok"], g)
                if first:
                    pe.wait_ge(S["wp_ok"], 4)
                pe.matmul(psQ[:, :], wqp[:, :], xT[:, :], start=True, stop=True).then_inc(S["q_ps"], 1)
                pe.wait_ge(S["cT_sb"], g + 1)
                if not first:
                    pe.wait_ge(S["khi_ok"], g)
                pe.matmul(psK[:, :], wkp[:, :], cT[:, :], start=True, stop=True).then_inc(S["k_ps"], 1)
                if not first:
                    pe.wait_ge(S["v_sb"], g)
                for b in range(G):
                    last = pe.matmul(psV[:, b * 128:(b + 1) * 128], cT[:, b * 128:(b + 1) * 128], wv_sb[:, :],
                                     start=True, stop=True)
                last.then_inc(S["v_ps"], 1)
                pe.wait_ge(S["q32_ok"], g + 1)
                if not first:
                    pe.wait_ge(S["sq_ok"], g)
                four(psN, lambda b: q32[:, b * 128:(b + 1) * 128]).then_inc(S["n_ps"], 1)
                if not first:
                    masks(g - 1)

            stage1(0)
            pe.wait_ge(S["w_step"], 2)
            pe.matmul(psW[:, 0:2], ones[:, :], wabs[:, :], start=True, stop=True).then_inc(S["wabs_ps"], 1)
            pe.wait_ge(S["w_step"], 12 + CT * TAPS)
            for i in range(4):
                if i:
                    pe.wait_ge(S["w_sb"], i)
                src = (lambda c: wtap[:, c, i, :]) if i < 3 else (lambda c: w2_n[:, c * 128:(c + 1) * 128])
                four(psW, src).then_inc(S["wtr_ps"], 1)

            with pe.Fori(1, NG) as g:
                stage1(g)
            norms(NG - 1)
            masks(NG - 1)

            pe.wait_ge(S["w_sb"], 4)
            pe.wait_ge(S["mask_ok"], NG)
            pe.wait_ge(S["sq_ok"], NG)
            pe.wait_ge(S["khi_ok"], NG)
            pe.wait_ge(S["v_sb"], NG)
            pe.wait_ge(S["const_v"], 4)

            def s_unit(s, j, n):
                b, half, q4 = n // 4, n % 2, n % 4 // 2
                N = UNITS * s + n
                if not (isinstance(s, int) and s == 0 and n < SRING):
                    pe.wait_ge(S["max_ok"], N - SRING + 1)
                p0 = 64 * half
                dst = sbank[(UNITS * j + n) % SRING]
                for i in range(4):
                    k = 4 * q4 + i
                    yield pe.matmul(dst[:, i * T:(i + 1) * T], qop[j][p0:p0 + KS, k, b * T:(b + 1) * T],
                                    kop[j][p0:p0 + KS, k, b * T:(b + 1) * T], start=True, stop=True)

            def t_unit(t, j, n):
                b, half, q4 = n // 4, (n + 1) % 2, n % 4 // 2
                N = UNITS * t + n
                if not (isinstance(t, int) and t == 0 and n < TRING):
                    pe.wait_ge(S["exp_ok"], N - TRING + 1)
                if n % 4 == 0:
                    pe.wait_ge(nm_in[b], 64 * (t + 1))
                p0 = 64 * half
                for i in range(4):
                    k = 4 * q4 + i
                    yield pe.matmul(tbank[n % TRING][:, i * T:(i + 1) * T], kop[j][p0:p0 + KT, k, b * T:(b + 1) * T],
                                    qop[j][p0:p0 + KT, k, b * T:(b + 1) * T], start=True, stop=True)

            def pv_of(t, j, n):
                b, half, q4 = n // 4, (n + 1) % 2, n % 4 // 2
                pe.wait_ge(S["exp_ok"], UNITS * t + n + 1)
                if n % 4 == 0 and not (isinstance(t, int) and t == 0 and n == 0):
                    pe.wait_ge(S["cU_ok"], 4 * t + b)
                w = 2 * half + q4
                for i in range(4):
                    h = HP * half + 4 * q4 + i
                    last = pe.matmul(pvbank[32 * i:32 * i + VW, w * T:(w + 1) * T], vop[j][:, b * H + h, :],
                                     probs[(UNITS * j + n) % PRING][:, i * T:(i + 1) * T], start=True, stop=True)
                last.then_inc(S["pv_unit"], 1)

            def natural(beta):
                pe.wait_ge(S["cU_ok"], beta + 1)
                pe.wait_ge(S["ctxn_ok"], beta)
                four(natbank, lambda w: ctxU[:, w * T:(w + 1) * T]).then_inc(S["nat_ps"], 1)

            def turn_max(sbatch, b):
                pe.wait_ge(S["max_ok"], 4 * (sbatch + 1))
                pe.transpose(mbank[0:H, 0:T], negmax[b % 2][:, :], ident[:, :]).then_inc(S["nm_ps"], 1)

            def turn_ctx(beta):
                pe.wait_ge(S["ctxn_ok"], beta + 1)
                pe.transpose(mbank[:, 0:T], ctxn[:, :, :].rearrange("p h d -> p (h d)"), ident[:, :])\
                    .then_inc(S["cT2_ps"], 1)

            def project(beta):
                pe.wait_ge(S["cT2_sb"], beta + 1)
                pe.matmul(mbank[:, 0:D], ctxT[:, :], wo_sb[:, :], start=True, stop=True).then_inc(S["proj_ps"], 1)

            def attend(s, sj, t, tj):
                tfirst = t is None or (isinstance(t, int) and t == 0)
                if s is not None:
                    if isinstance(s, int):
                        loads = s // NBUF
                    else:
                        loads = s_loads(s, sj)
                    pe.wait_ge(op_in[sj], 16 * LOADS * (loads + 1))
                for n in range(UNITS):
                    su = s_unit(s, sj, n) if s is not None else None
                    tu = t_unit(t, tj, n) if t is not None else None
                    for i in range(4):
                        if su is not None:
                            ms = next(su)
                        if tu is not None:
                            mt = next(tu)
                    if su is not None:
                        ms.then_inc(S["s_done"], 1)
                    if tu is not None:
                        mt.then_inc(S["t_done"], 1)
                        if n > 0:
                            pv_of(t, tj, n - 1)
                        elif not tfirst:
                            pv_of(t - 1, (tj - 1) % NBUF, UNITS - 1)
                    if n % 4 == 0 and t is not None and not (tfirst and n < 8):
                        project(4 * t + n // 4 - 2)
                    if n % 4 == 1:
                        if t is not None and not (tfirst and n < 4):
                            natural(4 * t + n // 4 - 1)
                        sbatch = (4 * s if s is not None else 4 * NG) + n // 4 - 1
                        if (s is not None or n == 1) and not (isinstance(s, int) and s == 0 and n < 4):
                            if t is not None and not (tfirst and n < 8):
                                pe.wait_ge(S["x1_ok"], 4 * t + n // 4 - 1)
                            elif not (isinstance(s, int) and s == 0 and n == 5):
                                pe.wait_ge(S["nm_ok"], sbatch)
                            turn_max(sbatch, (n // 4 - 1) % 4)
                    if n % 4 == 3 and t is not None and not (tfirst and n < 4):
                        if s is not None:
                            pe.wait_ge(S["nm_ok"], 4 * s + n // 4)
                        elif n == 3:
                            pe.wait_ge(S["nm_ok"], 4 * NG)
                        else:
                            pe.wait_ge(S["x1_ok"], 4 * t + n // 4 - 1)
                        turn_ctx(4 * t + n // 4 - 1)

            pe.wait_ge(S["const_v"], 3)
            attend(0, 0, None, None)
            attend(1, 1, 0, 0)
            with pe.Fori(0, 2) as r:
                s_loads = lambda s, sj: r + (1 if sj != 2 else 0)
                for j in range(3):
                    attend(3 * r + 2 + j, (2 + j) % NBUF, 3 * r + 1 + j, (1 + j) % NBUF)
            attend(None, None, 7, 1)
            pv_of(7, 1, UNITS - 1)
            project(4 * NG - 2)
            natural(4 * NG - 1)
            pe.wait_ge(S["x1_ok"], 4 * NG - 1)
            turn_ctx(4 * NG - 1)
            project(4 * NG - 1)

            pe.wait_ge(S["max_ok"], UNITS * NG)
            pe.wait_ge(S["exp_ok"], UNITS * NG)
            pe.wait_ge(S["x1_ok"], 4 * NG)
            pe.wait_ge(S["ctxn_ok"], 4 * NG)

            def stage3(g):
                first = isinstance(g, int) and g < 1
                pe.wait_ge(S["xq_ok"], g + 1)
                four(xqbank, lambda b: xn[:, b * 128:(b + 1) * 128]).then_inc(S["xqT_ps"], 1)
                pe.wait_ge(S["xqT_sb"], g + 1)
                for c in range(CT):
                    if not (first and c < 2):
                        pe.wait_ge(S["z_ok"], CT * g + c - 1)
                    for k in range(TAPS):
                        last = pe.matmul(ybank[c % 2][:, :], w1t[:, c, k, :], xqT[:, :, k:k + T],
                                         start=(k == 0), stop=(k == TAPS - 1))
                    last.then_inc(S["y_ps"], 1)
                pe.wait_ge(S["z_ok"], CT * (g + 1))
                for b in range(G):
                    if not (first and b < 2):
                        pe.wait_ge(S["zmax_ok"], G * g + b - 1)
                    four(ztbank[b % 2], lambda c: z[:, c, b * T:(b + 1) * T]).then_inc(S["zt_ps"], 1)
                pe.wait_ge(S["f_step"], (9 + 2 * G) * (g + 1))
                for b in range(G):
                    last = pe.matmul(scbank[:, b * T:(b + 1) * T], ones[:, :], diag[:, b, :], start=True, stop=True)
                last.then_inc(S["sc_ps"], 1)
                pe.wait_ge(S["zi_ok"], g + 1)
                if not first:
                    pe.wait_ge(S["o_ok"], g)
                for b in range(G):
                    for c in range(CT):
                        last = pe.matmul(obank[:, b * D:(b + 1) * D], zi[:, c, b * T:(b + 1) * T], w2t[:, c, :],
                                         start=(c == 0), stop=(c == CT - 1))
                last.then_inc(S["o_ps"], 1)

            stage3(0)
            with pe.Fori(1, NG) as g:
                stage3(g)


_INS = ["x", "ctx_1024", "L0_xattn_Wq", "L0_xattn_bq", "L0_xattn_Wk", "L0_xattn_bk", "L0_xattn_Wv", "L0_xattn_bv",
        "L0_xattn_Wo", "L0_xattn_bo", "L0_ffn_w1", "L0_ffn_conv_w", "L0_ffn_conv_b", "L0_ffn_w2"]


def kernel(**inputs):
    import numpy as _np
    import concourse.bacc as _bacc
    from concourse import mybir as _mybir
    from concourse.bass_utils import run_bass_kernel_spmd as _run

    nc = _bacc.Bacc("TRN2", target_bir_lowering=False, num_devices=1)
    arrays, args = {}, []
    for name in _INS:
        a = _np.ascontiguousarray(inputs[name])
        arrays[f"in_{name}_dram"] = a
        args.append(nc.dram_tensor(f"in_{name}_dram", a.shape, _mybir.dt.from_np(a.dtype), kind="ExternalInput").ap())
    args.append(nc.dram_tensor("out_0_dram", inputs["x"].shape, _mybir.dt.float32, kind="ExternalOutput").ap())
    xattn_ffn_kernel(nc, *args)
    r = _run(nc, [arrays], core_ids=[0])
    return r.results[0]["out_0_dram"]
```

```python
from contextlib import ExitStack

import concourse.bass as bass
from concourse import mybir

F32 = mybir.dt.float32
BF16 = mybir.dt.bfloat16
ALU = mybir.AluOpType
ACT = mybir.ActivationFunctionType
AX = mybir.AxisListType

ROUND = 1.5 * 2.0 ** 23
MASKED = -1.0e30
SMALLEST = 1e-5
EPS = 1e-5


def xattn_ffn_kernel(nc, x, ctx_in, Wq, bq, Wk, bk, Wv, bv, Wo, bo, w1, conv_w, conv_b, w2, out):
    B, T, D = x.shape
    H, DK = 16, 8
    HID = w1.shape[0]
    CT = HID // 128
    TAPS = conv_w.shape[2]
    G = 4
    NG = B // G
    GT = G * T
    GH = G * H
    NSEL = T // 2
    HP = H // 2
    PARTS = 3
    NPROD = 48
    KS = 126
    KT = 128
    VW = DK + 1
    UNITS = 16
    NBUF = 3
    SRING, TRING, PRING = 2, 2, 4
    SCALE = float(DK) ** -0.5
    NSETS = NG // 2
    LOADS = 14

    scr_q = nc.dram_tensor("scr_q", (NG, PARTS, D, GT), BF16).ap()
    scr_k = nc.dram_tensor("scr_k", (NG, PARTS, D, GT), BF16).ap()
    scr_m = nc.dram_tensor("scr_m", (NSETS, 2 * GH, T), BF16).ap()

    x_g = x.rearrange("(g b) t d -> g t b d", b=G)
    ctx_g = ctx_in.rearrange("(g b) t d -> g t b d", b=G)
    out_g = out.rearrange("(g b) t d -> g t b d", b=G)

    with ExitStack() as ctx:
        def sb(name, shape, dt):
            return ctx.enter_context(nc.sbuf_tensor(name, shape, dt))

        def sem(name):
            return ctx.enter_context(nc.semaphore(name))

        bank = [ctx.enter_context(nc.psum_tensor(f"bank{i}", [128, 512], F32)) for i in range(8)]

        ident = sb("ident", [128, 128], F32)
        ones = sb("ones", [128, 128], F32)
        minus_half = sb("minus_half", [128, G], F32)
        wq_sb = sb("wq_sb", [D, D], F32)
        wk_sb = sb("wk_sb", [D, D], F32)
        wqp = sb("wqp", [D, D], F32)
        wkp = sb("wkp", [D, D], F32)
        wv_sb = sb("wv_sb", [D, D], F32)
        wo_sb = sb("wo_sb", [D, D], F32)
        bq_c = sb("bq_c", [D, 1], F32)
        bk_c = sb("bk_c", [D, 1], F32)
        bv_r = sb("bv_r", [128, D], F32)
        bo_r = sb("bo_r", [128, D], F32)
        w1_n = sb("w1_n", [128, CT, D], F32)
        w2_n = sb("w2_n", [128, HID], F32)
        cw = sb("cw", [128, CT, TAPS], F32)
        cb = sb("cb", [128, CT], F32)
        wabs = sb("wabs", [128, 2], F32)
        wsc = sb("wsc", [128, 2], F32)
        winv = sb("winv", [128, 2], F32)
        x_all = sb("x_all", [128, B * D], F32)
        mask_all = sb("mask_all", [128, B * H], F32)

        qop = [[sb(f"qop{i}_{h}", [128, HP, GT], BF16) for h in range(2)] for i in range(NBUF)]
        kop = [sb(f"kop{i}", [128, HP, GT], BF16) for i in range(NBUF)]
        vop = [sb(f"vop{i}", [128, GH, VW], F32) for i in range(NBUF)]
        negmax = [sb(f"negmax{i}", [128, H], F32) for i in range(2)]
        nmT = [sb(f"nmT{i}", [H, 2, T], BF16) for i in range(2)]
        probs = [sb(f"probs{i}", [128, 512], F32) for i in range(PRING)]
        ctxU = sb("ctxU", [128, 512], F32)
        rden = sb("rden", [128, H], F32)
        rmask = sb("rmask", [128, H], F32)
        ctxn = sb("ctxn", [128, H, DK], F32)
        ctxT = sb("ctxT", [128, T], F32)
        v_all = sb("v_all", [128, NG * GH * VW], F32)
        w2t = sb("w2t", [128, CT, D], BF16)
        w1t = sb("w1t", [D, CT, TAPS, 128], F32)
        wtmp = sb("wtmp", [128, 512], F32)
        wtap = sb("wtap", [128, CT, TAPS, D], F32)

        stats = sb("stats", [128, G, 6], F32)
        mv = sb("mv", [128, G, 2], F32)
        vare = sb("vare", [128, G], F32)
        rstd = sb("rstd", [128, G], F32)
        xn = sb("xn", [128, GT], F32)

        whole, ctx = ctx, ExitStack()
        ctx_sb = [sb(f"ctx_sb{i}", [128, GT], F32) for i in range(2)]
        xT = sb("xT", [128, GT], F32)
        cT = sb("cT", [128, GT], F32)
        q32 = sb("q32", [128, GT], F32)
        k32 = sb("k32", [128, GT], F32)
        qr = sb("qr", [128, GT], F32)
        kr = sb("kr", [128, GT], F32)
        qp = [sb(f"qp{i}", [128, PARTS, GT], BF16) for i in range(2)]
        kp = [sb(f"kp{i}", [128, PARTS, GT], BF16) for i in range(2)]
        sq = sb("sq", [128, GT], F32)
        norm_all = sb("norm_all", [128, B * H], F32)
        work = sb("work", [128, NSETS, T], F32)
        top8 = sb("top8", [128, NSETS, 8], F32)
        maskT = sb("maskT", [128, NSETS, T], F32)
        negmask = sb("negmask", [128, NSETS, T], BF16)
        ctx.close()
        ctx = whole

        xn2 = sb("xn2", [128, G, D], F32)
        xr = sb("xr", [128, G, D], F32)
        amax = sb("amax", [128, G], F32)
        amaxc = sb("amaxc", [128, G], F32)
        arec = sb("arec", [128, G], F32)
        asc = sb("asc", [128, G], F32)
        ainv = sb("ainv", [128, G], F32)
        xqT = sb("xqT", [128, G, T + 2], F32)
        z = [sb(f"z{i}", [128, CT, GT], F32) for i in range(2)]
        zs = sb("zs", [128, CT, GT], F32)
        zi = sb("zi", [128, CT, GT], BF16)
        zmax = sb("zmax", [128, G], F32)
        zmaxc = sb("zmaxc", [128, G], F32)
        zrec = sb("zrec", [128, G], F32)
        zsc = sb("zsc", [128, G], F32)
        zinv = sb("zinv", [128, G], F32)
        zout = sb("zout", [128, G], F32)
        diag = sb("diag", [128, G, 128], F32)
        scb = sb("scb", [128, GT], F32)
        osb = sb("osb", [128, GT], F32)

        names = """k_step ones_in x1_in xr_in v_ok ops_free spare wp_ok const_p w_in w2_in const_z const_i const_v w_step wabs_ps t_step wtap_ok wtr_ps w_sb
            x_in ctx_in_s st_m
            stat_step var_ok rstd_ok xn_ok xT_ps cT_ps xT_sb cT_sb q_ps k_ps v_ps q32_ok qhi_ok k32_ok khi_ok
            n_ps sq_ok norm_ok nT_ps work_ok top_step maskT_ok negm_ok m_ps mask_ok v_sb
            qr_ok kr_ok qmid_ok kmid_ok qlo_ok klo_ok xbo_ok
            s_done max_ok t_done exp_ok pv_unit pv_b cU_ok nat_ps att_step ctxn_ok cT2_ps cT2_sb proj_ps x1_ok
            nm_ps nm_hi nm_ok
            stat3 var3 rstd3 f_step xq_ok xqT_ps xqT_sb y_ps z_ok zt_ps zmax_ok diag_ok sc_ps scb_ok
            zs_ok zi_ok o_ps o_ok out_st""".split()
        S = {n: sem(n) for n in names}
        op_in = [sem(f"op_in{i}") for i in range(NBUF)]
        st = {f: [sem(f"st_{f}{i}") for i in range(2)] for f in "qk"}
        ctx_s = [sem(f"ctx_s{i}") for i in range(2)]
        nm_in = [sem(f"nm_in{i}") for i in range(G)]

        def apart(eng, s, n):
            eng.wait_ge(s, n)
            eng.sem_inc(S["spare"], 1)

        def grp(t, g):
            return t[:, bass.ds(g * GT, GT)]

        block = ctx.enter_context(nc.Block())
        psX, psC, psQ, psK, psV, psN, psM, psW = bank
        sbank, tbank, nmbank, pvbank, natbank, mbank = bank[0:2], bank[2:4], bank[4], bank[5], bank[6], bank[7]
        ybank, ztbank, scbank, obank, xqbank = bank[0:2], bank[2:4], bank[4], bank[5], bank[6]

        @block.sync
        def _(sp):
            def load_x(g, n, inc):
                sp.dma_start(x_all[:, g * GT:(g + n) * GT].rearrange("p (b d) -> p b d", d=D),
                             x.rearrange("b t d -> t b d")[:, g * G:(g + n) * G]).then_inc(S[inc], 16)

            def load_ctx(g, buf):
                sp.dma_start(ctx_sb[buf][:, :].rearrange("p (b d) -> p b d", b=G), ctx_g[g]).then_inc(ctx_s[buf], 16)

            load_x(0, 1, "x_in")
            load_ctx(0, 0)
            for dst, src in ((wq_sb, Wq), (wk_sb, Wk), (wv_sb, Wv)):
                sp.dma_start(dst[:, :], src).then_inc(S["w_in"], 16)
            for dst, src in ((bq_c, bq), (bk_c, bk)):
                for h in range(2):
                    sp.dma_start(dst[64 * h:64 * h + 64, :],
                                 src.rearrange("(h k d a) -> h d k a", h=2, d=DK, a=1)[h],
                                 allow_slow_non_contiguous=True).then_inc(S["w_in"], 16)
            sp.dma_start(bv_r[:, :], bv.partition_broadcast(128)).then_inc(S["w_in"], 16)
            sp.dma_start(bo_r[:, :], bo.partition_broadcast(128)).then_inc(S["w_in"], 16)
            load_x(1, 1, "x1_in")
            load_ctx(1, 1)
            load_x(2, NG - 2, "xr_in")
            sp.dma_start(w1_n[:, :, :], w1.rearrange("(c p) d -> p c d", p=128)).then_inc(S["w2_in"], 16)
            sp.dma_start(w2_n[:, :], w2).then_inc(S["w2_in"], 16)
            sp.dma_start(cw[:, :, :], conv_w.rearrange("(c p) a k -> p c (a k)", p=128)).then_inc(S["w2_in"], 16)
            for c in range(CT):
                sp.dma_start(cb[:, c:c + 1], conv_b[c * 128:(c + 1) * 128].rearrange("(p a) -> p a", a=1))\
                    .then_inc(S["w2_in"], 16)
            sp.dma_start(wo_sb[:, :], Wo).then_inc(S["w2_in"], 16)

            def store(g, buf):
                for f, part, scr in (("q", qp, scr_q), ("k", kp, scr_k)):
                    for p in ("hi", "mid", "lo"):
                        sp.wait_ge(S[f + p + "_ok"], g + 1)
                    sp.dma_start(scr[g].rearrange("a p t -> p a t"), part[buf][:, :, :]).then_inc(st[f][buf], 16)

            for f in "qk":
                sp.sem_inc(st[f][0], 16)
                sp.sem_inc(st[f][1], 16)
            with sp.Fori(0, (NG - 2) // 2) as r:
                for u in range(2):
                    g = 2 * r + 1 + u
                    sp.wait_ge(S["cT_ps"], g)
                    load_ctx(g + 1, u)
                    store(g - 1, u)
            store(NG - 2, 0)
            store(NG - 1, 1)
            def load_ops(g, buf):
                for f in "qk":
                    for u in ((g,) if isinstance(g, int) and g < 2 else (0, 1)):
                        sp.wait_ge(st[f][u], 32 if isinstance(g, int) and g < 2 else 16 * (NG // 2 + 1))
                inc = op_in[buf]
                for half in range(2):
                    p0 = 64 * half
                    for dst, scr, is_k in ((qop[buf][half], scr_q, False), (kop[buf], scr_k, True)):
                        src = scr[g].rearrange("a (h d k) t -> h d a (k t)", h=2, d=DK)[half]
                        row = p0
                        for qpart, n in ((0, 3), (1, 2), (2, 1)):
                            if is_k:
                                s = src[:, 0:n]
                            else:
                                s = src[:, qpart:qpart + 1].broadcast_to([DK, n, HP * GT]) if n > 1 else src[:, qpart:qpart + 1]
                            sp.dma_start(dst[row:row + DK * n, :, :].rearrange("p k t -> p (k t)"), s).then_inc(inc, 16)
                            row += DK * n
                if isinstance(g, int) and g == 0:
                    sp.wait_ge(S["negm_ok"], 1)
                    sp.dma_start(scr_m.rearrange("m p t -> p m t"), negmask[:, :, :]).then_inc(S["st_m"], 16)
                    sp.wait_ge(S["st_m"], 16)
                for half in range(2):
                    p0 = 64 * half
                    sp.dma_start(kop[buf][p0 + NPROD:p0 + NPROD + 1, :, :].rearrange("p k (b t) -> p k b t", b=G),
                                 scr_m.rearrange("m (e b h k) t -> (m e) h k b t", e=2, b=G, h=2)[g][half:half + 1])\
                        .then_inc(inc, 16)

            def move_max(s, b, buf):
                sp.wait_ge(S["nm_ok"], 4 * s + b + 1)
                for half in range(2):
                    for part in range(2):
                        row = KS + part
                        sp.dma_start(qop[buf][half][row:row + 1, :, b * T:(b + 1) * T],
                                     nmT[b % 2][HP * half:HP * half + HP, part, :]).then_inc(nm_in[b], 16)

            sp.wait_ge(S["const_p"], 3 * NBUF)
            for i in range(NBUF):
                for half in range(2):
                    row = 64 * half + NPROD
                    sp.dma_start(qop[i][half][row:row + 1, :, :].rearrange("p k t -> p (k t)"),
                                 kop[2][0:1, :, :].rearrange("p k t -> p (k t)")).then_inc(S["ones_in"], 16)
            load_ops(0, 0)
            load_ops(1, 1)
            for b in range(3):
                move_max(0, b, 0)
            sp.wait_ge(S["ones_in"], 16 * 2 * NBUF)
            sp.sem_inc(S["ops_free"], 1)
            with sp.Fori(0, 2) as r:
                for j in range(NBUF):
                    s = 3 * r + 2 + j
                    sp.wait_ge(S["ops_free"], s - 1)
                    load_ops(s, (2 + j) % NBUF)
                    move_max(s - 2, 3, j % NBUF)
                    for b in range(3):
                        move_max(s - 1, b, (1 + j) % NBUF)
            move_max(6, 3, 0)
            for b in range(4):
                move_max(7, b, 1)

            def store_out(g):
                sp.wait_ge(S["o_ok"], g + 1)
                sp.dma_start(out_g[g], osb[:, :].rearrange("p (b d) -> p b d", b=G)).then_inc(S["out_st"], 16)
            with sp.Fori(0, NG) as g:
                store_out(g)
            sp.wait_ge(S["out_st"], 16 * NG)

        @block.gpsimd
        def _(pool):
            pool.memset(ident[:, :], 0.0).then_inc(S["const_z"], 1)
            pool.wait_ge(S["const_z"], 1)
            pool.affine_select(out=ident[:, :], in_=ident[:, :], compare_op=ALU.not_equal, fill=1.0, base=0,
                               pattern=[[-1, 128]], channel_multiplier=1).then_inc(S["const_i"], 1)
            pool.memset(minus_half[:, :], -0.5).then_inc(S["const_z"], 1)
            pool.wait_ge(S["const_z"], 2)
            def inv_std(ok_in, ok_out, n):
                pool.wait_ge(ok_in, n)
                pool.tensor_tensor(rstd[:, :], vare[:, :], minus_half[:, :], ALU.pow).then_inc(ok_out, 1)

            def rest(g, u):
                for f, part, r, t in (("q", qp, qr, q32), ("k", kp, kr, k32)):
                    pool.wait_ge(S[f + "hi_ok"], g + 1)
                    pool.wait_ge(S[f + "32_ok"], g + 1)
                    if not (isinstance(g, int) and g < 1):
                        pool.wait_ge(S[f + "lo_ok"], g)
                    pool.tensor_tensor(r[:, :], t[:, :], part[u][:, 0, :], ALU.subtract).then_inc(S[f + "r_ok"], 1)

            def low(g, u):
                for f, part, r in (("q", qp, qr), ("k", kp, kr)):
                    pool.wait_ge(S[f + "mid_ok"], g + 1)
                    pool.tensor_tensor(part[u][:, 2, :], r[:, :], part[u][:, 1, :], ALU.subtract).then_inc(S[f + "lo_ok"], 1)

            def stage1(g, u, more):
                if more:
                    inv_std(S["var_ok"], S["rstd_ok"], g + 2)
                if not (isinstance(g, int) and g < 1):
                    low(g - 1, 1 - u)
                rest(g, u)

            inv_std(S["var_ok"], S["rstd_ok"], 1)
            pool.wait_ge(S["w_in"], 16 * 9)
            stage1(0, 0, True)
            for k in kop:
                pool.memset(k[:, :, :].rearrange("p k t -> p (k t)"), 1.0).then_inc(S["const_p"], 1)
            with pool.Fori(0, (NG - 2) // 2) as r:
                for u in range(2):
                    stage1(2 * r + 1 + u, 1 - u, True)
            stage1(NG - 1, 1, False)
            low(NG - 1, 1)
            pool.wait_ge(S["xn_ok"], NG)
            xb = x_all[:, :].rearrange("p (b d) -> p b d", b=B)
            pool.tensor_tensor(xb, xb, bo_r[:, :].unsqueeze(1).broadcast_to([128, B, D]), ALU.add).then_inc(S["xbo_ok"], 1)

            pool.wait_ge(S["w_step"], 5)
            tstep = [0]

            def chain(ins):
                tstep[0] += 1
                ins.then_inc(S["t_step"], 1)
                pool.wait_ge(S["t_step"], tstep[0])

            w1f = w1_n[:, :, :].rearrange("p c d -> p (c d)")
            for wf, k in ((w1f, 0), (w2_n[:, :], 1)):
                chain(pool.tensor_scalar(wtmp[:, :], wf, wsc[:, k:k + 1], ROUND, ALU.mult, ALU.add))
                chain(pool.tensor_scalar(wtmp[:, :], wtmp[:, :], ROUND, 1.0, ALU.subtract, ALU.min))
                chain(pool.tensor_scalar(wf, wtmp[:, :], -1.0, None, ALU.max))
            chain(pool.tensor_scalar(w1f, w1f, winv[:, 0:1], None, ALU.mult))
            for c in range(CT):
                for k in range(TAPS):
                    pool.tensor_scalar(wtap[:, c, k, :], w1_n[:, c, :], cw[:, c, k:k + 1], None, ALU.mult)\
                        .then_inc(S["wtap_ok"], 1)

            def scaled(k, u):
                pool.wait_ge(S["scb_ok"], k + 1)
                if not (isinstance(k, int) and k < 1):
                    pool.wait_ge(S["zi_ok"], k)
                for c in range(CT):
                    pool.tensor_tensor(zs[:, c, :], z[u][:, c, :], scb[:, :], ALU.mult).then_inc(S["zs_ok"], 1)

            inv_std(S["var3"], S["rstd3"], 1)
            inv_std(S["var3"], S["rstd3"], 2)
            inv_std(S["var3"], S["rstd3"], 3)
            scaled(0, 0)
            with pool.Fori(0, (NG - 4) // 2) as r:
                for u in range(2):
                    inv_std(S["var3"], S["rstd3"], 2 * r + u + 4)
                    scaled(2 * r + 1 + u, 1 - u)
            inv_std(S["var3"], S["rstd3"], NG)
            scaled(NG - 3, 1)
            scaled(NG - 2, 0)
            scaled(NG - 1, 1)

        @block.scalar
        def _(act):
            act.wait_ge(S["w_in"], 16 * 9)

            def parts(g, u, turn, f, ps, t32, part, bias):
                act.wait_ge(S[f + "_ps"], g + 1)
                if not (isinstance(g, int) and g < 1):
                    act.wait_ge(S[f + "r_ok"], g)
                    act.wait_ge(S["n_ps"], g)
                    act.wait_ge(st[f][u], 16 * turn)
                act.activation(t32[:, :], ps[:, :], ACT.Identity, bias=bias[:, 0:1]).then_inc(S[f + "32_ok"], 1)
                act.activation(part[u][:, 0, :], ps[:, :], ACT.Identity, bias=bias[:, 0:1]).then_inc(S[f + "hi_ok"], 1)

            def squares(g):
                act.wait_ge(S["n_ps"], g + 1)
                act.wait_ge(S["norm_ok"], g + 1)
                act.activation(sq[:, :], psN[:, :], ACT.Square).then_inc(S["sq_ok"], 1)

            def middle(g, u):
                for f, part, r in (("q", qp, qr), ("k", kp, kr)):
                    act.wait_ge(S[f + "r_ok"], g + 1)
                    act.activation(part[u][:, 1, :], r[:, :], ACT.Copy).then_inc(S[f + "mid_ok"], 1)

            def stage1(g, u, turn):
                act.wait_ge(S["xT_ps"], g + 1)
                act.activation(xT[:, :], psX[:, :], ACT.Copy).then_inc(S["xT_sb"], 1)
                act.wait_ge(S["cT_ps"], g + 1)
                if not (isinstance(g, int) and g < 1):
                    act.wait_ge(S["v_ps"], g)
                act.activation(cT[:, :], psC[:, :], ACT.Copy).then_inc(S["cT_sb"], 1)
                if not (isinstance(g, int) and g < 1):
                    middle(g - 1, 1 - u)
                    squares(g - 1)
                parts(g, u, turn, "q", psQ, q32, qp, bq_c)
                parts(g, u, turn, "k", psK, k32, kp, bk_c)

            stage1(0, 0, 1)
            with act.Fori(0, (NG - 2) // 2) as r:
                stage1(2 * r + 1, 1, r + 1)
                stage1(2 * r + 2, 0, r + 2)
            stage1(NG - 1, 1, NG // 2)
            middle(NG - 1, 1)
            squares(NG - 1)

            def attend(t, j):
                first = isinstance(t, int) and t == 0
                act.activation(vop[j][:, :, :].rearrange("p h c -> p (h c)"),
                               v_all[:, bass.ds(t * (GH * VW), GH * VW)], ACT.Copy).then_inc(S["v_ok"], 1)
                for n in range(UNITS):
                    N = UNITS * t + n
                    act.wait_ge(S["t_done"], N + 1)
                    if not (first and n < PRING):
                        act.wait_ge(S["pv_unit"], N - PRING + 1)
                    act.activation(probs[(UNITS * j + n) % PRING][:, :], tbank[n % TRING][:, :], ACT.Exp,
                                   scale=SCALE).then_inc(S["exp_ok"], 1)
                    beta = 4 * t + n // 4 - 1
                    if not (first and n < 4):
                        if n % 4 == 0:
                            context(beta)
                        if n == 0:
                            act.sem_inc(S["ops_free"], 1)
                        if n % 4 == 3:
                            turned(beta)

            def context(beta):
                act.wait_ge(S["pv_unit"], 4 * (beta + 1))
                act.wait_ge(S["nat_ps"], beta)
                act.activation(ctxU[:, :], pvbank[:, :], ACT.Copy).then_inc(S["cU_ok"], 1)

            def turned(beta):
                act.wait_ge(S["cT2_ps"], beta + 1)
                act.wait_ge(S["proj_ps"], beta)
                act.activation(ctxT[:, :], mbank[:, 0:T], ACT.Copy).then_inc(S["cT2_sb"], 1)

            act.wait_ge(S["v_sb"], NG)
            attend(0, 0)
            with act.Fori(0, 2) as r:
                for j in range(3):
                    attend(3 * r + 1 + j, (1 + j) % NBUF)
            attend(7, 1)
            context(4 * NG - 1)
            turned(4 * NG - 1)

            def stage3(f, fu, k):
                def silu(c):
                    act.wait_ge(S["y_ps"], CT * f + c + 1)
                    if c == 0 and not (isinstance(f, int) and f < 2):
                        act.wait_ge(S["zs_ok"], CT * (f - 1))
                    act.activation(z[fu][:, c, :], ybank[c % 2][:, :], ACT.Silu, bias=cb[:, c:c + 1]).then_inc(S["z_ok"], 1)

                if f is not None:
                    act.wait_ge(S["xqT_ps"], f + 1)
                    if not (isinstance(f, int) and f < 1):
                        act.wait_ge(S["y_ps"], CT * f)
                    act.activation(xqT[:, :, 1:T + 1], xqbank[:, :].rearrange("p (b t) -> p b t", b=G),
                                   ACT.Copy).then_inc(S["xqT_sb"], 1)
                    silu(0)
                    silu(1)
                if k is not None:
                    act.wait_ge(S["sc_ps"], k + 1)
                    if not (isinstance(k, int) and k < 1):
                        act.wait_ge(S["zs_ok"], CT * k)
                    act.activation(scb[:, :], scbank[:, :], ACT.Copy).then_inc(S["scb_ok"], 1)
                if f is not None:
                    silu(2)
                    silu(3)

            for i in range(TAPS + 1):
                act.wait_ge(S["wtr_ps"], i + 1)
                dst = w1t[:, :, i, :] if i < TAPS else w2t[:, :, :]
                act.activation(dst, bank[i][:, :].rearrange("p (c k) -> p c k", c=CT), ACT.Copy).then_inc(S["w_sb"], 1)
            act.wait_ge(S["w2_in"], 16 * (4 + CT))
            stage3(0, 0, None)
            stage3(1, 1, 0)
            with act.Fori(0, (NG - 2) // 2) as r:
                for u in range(2):
                    stage3(2 * r + 2 + u, u, 2 * r + 1 + u)
            stage3(None, None, NG - 1)

        @block.vector
        def _(dve):
            dve.sem_inc(S["norm_ok"], 1)
            dve.sem_inc(S["sq_ok"], 1)
            dve.memset(ones[:, :], 1.0).then_inc(S["const_v"], 1)
            dve.memset(v_all[:, :].rearrange("p (h c) -> p h c", c=VW)[:, :, DK:VW], 1.0).then_inc(S["const_v"], 1)

            def clear(q):
                dve.memset(q[:, :, :].rearrange("p k t -> p (k t)"), 0.0).then_inc(S["const_p"], 1)
            clear(qop[0][0])

            def stats_of(g, step, ok, count):
                for b in range(G):
                    dve.bn_stats(stats[:, b, :], x_all[:, bass.ds(g * GT + b * D, D)]).then_inc(step, 1)
                apart(dve, step, count * 2 * G + G)
                for b in range(G):
                    dve.bn_aggr(mv[:, b, :], stats[:, b, :]).then_inc(step, 1)
                dve.wait_ge(step, (count + 1) * 2 * G)
                dve.tensor_scalar(vare[:, :], mv[:, :, 1], EPS, None, ALU.add).then_inc(ok, 1)

            def normalise(g, dst):
                for b in range(G):
                    last = dve.tensor_scalar(dst[:, b * D:(b + 1) * D], x_all[:, bass.ds(g * GT + b * D, D)],
                                             mv[:, b, 0:1], rstd[:, b:b + 1], ALU.subtract, ALU.mult)
                return last

            def select():
                step = S["top_step"]
                dve.wait_ge(S["nT_ps"], NSETS)
                dve.tensor_copy(work[:, :, :].rearrange("p m t -> p (m t)"), psM[:, :]).then_inc(step, 1)
                for i in range(NSEL // 8):
                    for m in range(NSETS):
                        dve.wait_ge(step, 1 if i == 0 else 2 + 2 * NSETS * i - NSETS + m)
                        dve.max(top8[:, m, :], work[:, m, :]).then_inc(step, 1)
                    for m in range(NSETS):
                        dve.wait_ge(step, 2 + 2 * NSETS * i + m)
                        dve.match_replace(work[:, m, :], top8[:, m, :], work[:, m, :], -1.0).then_inc(step, 1)
                dve.wait_ge(step, 1 + 2 * NSETS * (NSEL // 8))
                dve.tensor_scalar(negmask[:, :, :], work[:, :, :], 0.0, MASKED, ALU.is_ge, ALU.mult).then_inc(S["negm_ok"], 1)
                dve.tensor_scalar(maskT[:, :, :], work[:, :, :], 0.0, None, ALU.is_lt).then_inc(S["maskT_ok"], 1)
                dve.wait_ge(S["m_ps"], NSETS)
                dve.tensor_copy(mask_all[:, :], psW[:, :]).then_inc(S["mask_ok"], 1)

            def values(g):
                dve.wait_ge(S["v_ps"], g + 1)
                dve.tensor_tensor(v_all[:, bass.ds(g * (GH * VW), GH * VW)].rearrange("p (b h c) -> p b h c", b=G, c=VW)[:, :, :, 0:DK],
                                  psV[:, :].rearrange("p (b h c) -> p b h c", b=G, c=DK),
                                  bv_r[:, :].rearrange("p (h c) -> p h c", c=DK).unsqueeze(1).broadcast_to([128, G, H, DK]),
                                  ALU.add).then_inc(S["v_sb"], 1)

            def norms(g):
                dve.wait_ge(S["sq_ok"], g + 2)
                dve.tensor_reduce(norm_all[:, bass.ds(g * GH, GH)],
                                  sq[:, :].rearrange("p (h d k) -> p h k d", d=DK, k=HP), AX.X, ALU.add)\
                    .then_inc(S["norm_ok"], 1)

            def stage1(g, x_sem):
                dve.wait_ge(S["rstd_ok"], g + 1)
                if not (isinstance(g, int) and g < 1):
                    dve.wait_ge(S["xT_ps"], g)
                normalise(g, xn).then_inc(S["xn_ok"], 1)
                if not (isinstance(g, int) and g < 1):
                    values(g - 1)
                if x_sem is not None:
                    dve.wait_ge(S[x_sem], 16)
                    dve.wait_ge(S["xn_ok"], g + 1)
                    stats_of(g + 1, S["stat_step"], S["var_ok"], g + 1)
                if not (isinstance(g, int) and g < 1):
                    norms(g - 1)

            dve.wait_ge(S["const_v"], 2)
            dve.wait_ge(S["x_in"], 16)
            stats_of(0, S["stat_step"], S["var_ok"], 0)
            dve.wait_ge(S["w_in"], 16 * 9)
            for dst, src in ((wqp, wq_sb), (wkp, wk_sb)):
                for h in range(2):
                    dve.tensor_copy(dst[:, 64 * h:64 * h + 64].rearrange("p (d k) -> p d k", d=DK),
                                    src[:, 64 * h:64 * h + 64].rearrange("p (k d) -> p d k", d=DK)).then_inc(S["wp_ok"], 1)
            stage1(0, "x1_in")

            for q in (qop[0][1], qop[1][0], qop[1][1]):
                clear(q)

            wstep = [0]

            def chain(ins):
                wstep[0] += 1
                ins.then_inc(S["w_step"], 1)
                dve.wait_ge(S["w_step"], wstep[0])

            dve.wait_ge(S["w2_in"], 16 * (4 + CT))
            chain(dve.tensor_reduce(wabs[:, 0:1], w1_n[:, :, :], AX.XY, ALU.add, apply_absolute_value=True))
            chain(dve.tensor_reduce(wabs[:, 1:2], w2_n[:, :], AX.X, ALU.add, apply_absolute_value=True))
            dve.wait_ge(S["wabs_ps"], 1)
            chain(dve.tensor_scalar(wabs[:, :], psW[:, 0:2], 1.0 / (HID * D), SMALLEST, ALU.mult, ALU.max))
            chain(dve.reciprocal(wsc[:, :], wabs[:, :]))
            chain(dve.reciprocal(winv[:, :], wsc[:, :]))

            with dve.Fori(1, NG - 1) as g:
                stage1(g, "xr_in")
            clear(qop[2][0])
            clear(qop[2][1])
            stage1(NG - 1, None)
            values(NG - 1)
            norms(NG - 1)
            select()

            def maximum(s, j, n):
                N = UNITS * s + n
                dve.wait_ge(S["s_done"], N + 1)
                b, half, q4 = n // 4, n % 2, n % 4 // 2
                if n % 4 == 0 and not (isinstance(s, int) and s == 0 and n < 8):
                    dve.wait_ge(S["nm_ps"], 4 * s + b - 1)
                h0 = HP * half + 4 * q4
                dve.tensor_reduce(negmax[b % 2][:, h0:h0 + 4],
                                  sbank[(UNITS * j + n) % SRING][:, :].rearrange("p (h k) -> p h k", h=4),
                                  AX.X, ALU.max, negate=True).then_inc(S["max_ok"], 1)

            def split_max(sb_index, b):
                dve.wait_ge(S["nm_ps"], sb_index + 1)
                dve.tensor_copy(nmT[b % 2][:, 0, :], nmbank[0:H, 0:T]).then_inc(S["nm_hi"], 1)
                dve.wait_ge(S["nm_hi"], sb_index + 1)
                dve.tensor_tensor(nmT[b % 2][:, 1, :], nmbank[0:H, 0:T], nmT[b % 2][:, 0, :],
                                  ALU.subtract).then_inc(S["nm_ok"], 1)

            def weigh(beta):
                dve.wait_ge(S["nat_ps"], beta + 1)
                nat = natbank[:, :].rearrange("p (h r) -> p h r", r=32)
                dve.reciprocal(rden[:, :], nat[:, :, DK]).then_inc(S["att_step"], 1)
                dve.wait_ge(S["att_step"], 2 * beta + 1)
                dve.tensor_tensor(rmask[:, :], rden[:, :], mask_all[:, bass.ds(beta * H, H)], ALU.mult)\
                    .then_inc(S["att_step"], 1)
                dve.wait_ge(S["att_step"], 2 * beta + 2)
                dve.wait_ge(S["cT2_ps"], beta)
                dve.tensor_tensor(ctxn[:, :, :], nat[:, :, 0:DK], rmask[:, :].unsqueeze(2).broadcast_to([128, H, DK]),
                                  ALU.mult).then_inc(S["ctxn_ok"], 1)

            def residual(beta):
                dve.wait_ge(S["proj_ps"], beta + 1)
                xb = x_all[:, bass.ds(beta * D, D)]
                dve.tensor_tensor(xb, mbank[:, 0:D], xb, ALU.add).then_inc(S["x1_ok"], 1)

            def attend(s, sj, t):
                for n in range(UNITS):
                    if s is not None:
                        maximum(s, sj, n)
                    if n % 4 == 1 and t is not None and not (isinstance(t, int) and t == 0 and n < 8):
                        residual(4 * t + n // 4 - 2)
                    if n % 4 == 2 and t is not None and not (isinstance(t, int) and t == 0 and n < 4):
                        weigh(4 * t + n // 4 - 1)
                    if n % 4 == 3:
                        sbatch = (4 * s if s is not None else 4 * NG) + n // 4 - 1
                        b = (n // 4 - 1) % 4
                        if (s is not None or n == 3) and not (isinstance(s, int) and s == 0 and n < 4):
                            if not (isinstance(s, int) and (s == 0 and b < 2)):
                                prev = (b - 2) % 4
                                rounds = (s if s is not None else NG) - (1 if n < 4 else 0) - (1 if b < 2 else 0)
                                if not (isinstance(rounds, int) and rounds < 0):
                                    dve.wait_ge(nm_in[prev], 64 * (rounds + 1))
                            split_max(sbatch, b)

            dve.memset(pvbank[:, :], 0.0).then_inc(S["const_v"], 1)
            dve.wait_ge(S["xbo_ok"], 1)
            attend(0, 0, None)
            attend(1, 1, 0)
            with dve.Fori(0, 2) as r:
                for j in range(3):
                    attend(3 * r + 2 + j, (2 + j) % NBUF, 3 * r + 1 + j)
            attend(None, None, 7)
            residual(4 * NG - 2)
            weigh(4 * NG - 1)
            residual(4 * NG - 1)

            NA = 6 + G

            def f(g, n):
                dve.wait_ge(S["f_step"], NA * g + n)

            def stats3(g):
                stats_of(g, S["stat3"], S["var3"], g)

            def quantise(g):
                dve.wait_ge(S["rstd3"], g + 1)
                normalise(g, xn2[:, :, :].rearrange("p b d -> p (b d)")).then_inc(S["f_step"], 1)
                f(g, 1)
                dve.tensor_reduce(amax[:, :], xn2[:, :, :], AX.X, ALU.max, apply_absolute_value=True).then_inc(S["f_step"], 1)
                f(g, 2)
                dve.tensor_scalar(amaxc[:, :], amax[:, :], SMALLEST, None, ALU.max).then_inc(S["f_step"], 1)
                f(g, 3)
                dve.reciprocal(arec[:, :], amaxc[:, :]).then_inc(S["f_step"], 1)
                f(g, 4)
                dve.tensor_scalar(asc[:, :], arec[:, :], 127.0, None, ALU.mult).then_inc(S["f_step"], 1)
                f(g, 5)
                dve.reciprocal(ainv[:, :], asc[:, :]).then_inc(S["f_step"], 1)
                for b in range(G):
                    dve.tensor_scalar(xr[:, b, :], xn2[:, b, :], asc[:, b:b + 1], ROUND, ALU.mult, ALU.add)\
                        .then_inc(S["f_step"], 1)
                f(g, NA)
                if not (isinstance(g, int) and g < 1):
                    dve.wait_ge(S["xqT_ps"], g)
                for b in range(G):
                    last = dve.tensor_scalar(xn[:, b * D:(b + 1) * D], xr[:, b, :], ROUND, ainv[:, b:b + 1],
                                             ALU.subtract, ALU.mult)
                last.then_inc(S["xq_ok"], 1)

            NK = 5

            def ranges(k):
                for b in range(G):
                    dve.wait_ge(S["zt_ps"], G * k + b + 1)
                    dve.tensor_reduce(zmax[:, b:b + 1], ztbank[b % 2][:, :], AX.X, ALU.max, apply_absolute_value=True)\
                        .then_inc(S["zmax_ok"], 1)
                dve.wait_ge(S["zmax_ok"], G * (k + 1))
                dve.tensor_scalar(zmaxc[:, :], zmax[:, :], SMALLEST, None, ALU.max).then_inc(S["k_step"], 1)
                dve.wait_ge(S["k_step"], NK * k + 1)
                dve.reciprocal(zrec[:, :], zmaxc[:, :]).then_inc(S["k_step"], 1)
                dve.wait_ge(S["k_step"], NK * k + 2)
                dve.tensor_scalar(zsc[:, :], zrec[:, :], 127.0, None, ALU.mult).then_inc(S["k_step"], 1)
                dve.wait_ge(S["k_step"], NK * k + 3)
                for b in range(G):
                    last = dve.tensor_scalar(diag[:, b, :], ident[:, :], zsc[:, b:b + 1], None, ALU.mult)
                last.then_inc(S["diag_ok"], 1)
                dve.reciprocal(zinv[:, :], zsc[:, :]).then_inc(S["k_step"], 1)
                dve.wait_ge(S["k_step"], NK * k + 4)
                dve.tensor_scalar(zout[:, :], zinv[:, :], winv[:, 1:2], None, ALU.mult).then_inc(S["k_step"], 1)

            def rounded(k):
                if not (isinstance(k, int) and k < 1):
                    dve.wait_ge(S["o_ps"], k)
                for c in range(CT):
                    dve.wait_ge(S["zs_ok"], CT * k + c + 1)
                    last = dve.tensor_scalar(zi[:, c, :], zs[:, c, :], ROUND, ROUND, ALU.add, ALU.subtract)
                last.then_inc(S["zi_ok"], 1)

            def result(k):
                dve.wait_ge(S["o_ps"], k + 1)
                dve.wait_ge(S["k_step"], NK * (k + 1))
                if not (isinstance(k, int) and k < 1):
                    dve.wait_ge(S["out_st"], 16 * k)
                for b in range(G):
                    last = dve.scalar_tensor_tensor(out=osb[:, b * D:(b + 1) * D], in0=obank[:, b * D:(b + 1) * D],
                                                    scalar=zout[:, b:b + 1], in1=x_all[:, bass.ds(k * GT + b * D, D)],
                                                    op0=ALU.mult, op1=ALU.add)
                last.then_inc(S["o_ok"], 1)

            def stage3(a, k):
                if a is not None:
                    stats3(a)
                ranges(k)
                if a is not None:
                    quantise(a)
                rounded(k)
                result(k)

            dve.wait_ge(S["x1_ok"], B)
            dve.memset(xqT[:, :, :], 0.0).then_inc(S["const_v"], 1)
            stats3(0)
            quantise(0)
            stats3(1)
            quantise(1)
            stage3(2, 0)
            with dve.Fori(1, NG - 2) as k:
                stage3(k + 2, k)
            stage3(None, NG - 2)
            stage3(None, NG - 1)

        @block.tensor
        def _(pe):
            pe.wait_ge(S["const_i"], 1)
            pe.wait_ge(S["const_v"], 2)
            pe.wait_ge(S["w_in"], 16 * 9)

            def four(dst, src):
                for b in range(4):
                    last = pe.transpose(dst[:, b * 128:(b + 1) * 128], src(b), ident[:, :])
                return last

            def turn_q(g):
                pe.wait_ge(S["q32_ok"], g + 1)
                pe.wait_ge(S["sq_ok"], g + 1)
                four(psN, lambda b: q32[:, b * 128:(b + 1) * 128]).then_inc(S["n_ps"], 1)

            def stage1(g, u, turn):
                first = isinstance(g, int) and g < 1
                pe.wait_ge(S["xn_ok"], g + 1)
                four(psX, lambda b: xn[:, b * 128:(b + 1) * 128]).then_inc(S["xT_ps"], 1)
                pe.wait_ge(ctx_s[u], 16 * turn)
                four(psC, lambda b: ctx_sb[u][:, b * 128:(b + 1) * 128]).then_inc(S["cT_ps"], 1)
                if not first:
                    turn_q(g - 1)
                pe.wait_ge(S["xT_sb"], g + 1)
                if not first:
                    pe.wait_ge(S["qhi_ok"], g)
                if first:
                    pe.wait_ge(S["wp_ok"], 4)
                pe.matmul(psQ[:, :], wqp[:, :], xT[:, :], start=True, stop=True).then_inc(S["q_ps"], 1)
                pe.wait_ge(S["cT_sb"], g + 1)
                if not first:
                    pe.wait_ge(S["khi_ok"], g)
                pe.matmul(psK[:, :], wkp[:, :], cT[:, :], start=True, stop=True).then_inc(S["k_ps"], 1)
                if not first:
                    pe.wait_ge(S["v_sb"], g)
                for b in range(G):
                    last = pe.matmul(psV[:, b * 128:(b + 1) * 128], cT[:, b * 128:(b + 1) * 128], wv_sb[:, :],
                                     start=True, stop=True)
                last.then_inc(S["v_ps"], 1)

            stage1(0, 0, 1)
            pe.wait_ge(S["w_step"], 2)
            pe.matmul(psW[:, 0:2], ones[:, :], wabs[:, :], start=True, stop=True).then_inc(S["wabs_ps"], 1)

            with pe.Fori(0, (NG - 2) // 2) as r:
                stage1(2 * r + 1, 1, r + 1)
                stage1(2 * r + 2, 0, r + 2)
            stage1(NG - 1, 1, NG // 2)
            turn_q(NG - 1)
            pe.wait_ge(S["norm_ok"], NG + 1)
            for m in range(NSETS):
                pe.transpose(psM[:, m * T:(m + 1) * T], norm_all[:, m * 2 * GH:(m + 1) * 2 * GH], ident[:, :])\
                    .then_inc(S["nT_ps"], 1)
            pe.wait_ge(S["maskT_ok"], 1)
            pe.wait_ge(S["w_step"], 3)
            for m in range(NSETS):
                pe.transpose(psW[:, m * 128:(m + 1) * 128], maskT[:, m, :], ident[:, :]).then_inc(S["m_ps"], 1)

            pe.wait_ge(S["mask_ok"], 1)
            pe.wait_ge(S["ones_in"], 16 * 2 * NBUF)
            pe.wait_ge(S["w2_in"], 16 * (4 + CT))
            pe.wait_ge(S["sq_ok"], NG + 1)
            pe.wait_ge(S["khi_ok"], NG)
            pe.wait_ge(S["v_sb"], NG)
            pe.wait_ge(S["const_v"], 3)

            def s_unit(s, j, n):
                b, half, q4 = n // 4, n % 2, n % 4 // 2
                N = UNITS * s + n
                if not (isinstance(s, int) and s == 0 and n < SRING):
                    pe.wait_ge(S["max_ok"], N - SRING + 1)
                dst = sbank[(UNITS * j + n) % SRING]
                for i in range(4):
                    k = 4 * q4 + i
                    yield pe.matmul(dst[:, i * T:(i + 1) * T], qop[j][half][0:KS, k, b * T:(b + 1) * T],
                                    kop[j][0:KS, k, b * T:(b + 1) * T], start=True, stop=True)

            def t_unit(t, j, n):
                b, half, q4 = n // 4, (n + 1) % 2, n % 4 // 2
                N = UNITS * t + n
                if not (isinstance(t, int) and t == 0 and n < TRING):
                    pe.wait_ge(S["exp_ok"], N - TRING + 1)
                if n % 4 == 0:
                    pe.wait_ge(nm_in[b], 64 * (t + 1))
                for i in range(4):
                    k = 4 * q4 + i
                    yield pe.matmul(tbank[n % TRING][:, i * T:(i + 1) * T], kop[j][0:KT, k, b * T:(b + 1) * T],
                                    qop[j][half][0:KT, k, b * T:(b + 1) * T], start=True, stop=True)

            def pv_of(t, j, n):
                b, half, q4 = n // 4, (n + 1) % 2, n % 4 // 2
                pe.wait_ge(S["exp_ok"], UNITS * t + n + 1)
                if n % 4 == 0 and not (isinstance(t, int) and t == 0 and n == 0):
                    pe.wait_ge(S["cU_ok"], 4 * t + b)
                w = 2 * half + q4
                for i in range(4):
                    h = HP * half + 4 * q4 + i
                    last = pe.matmul(pvbank[32 * i:32 * i + VW, w * T:(w + 1) * T], vop[j][:, b * H + h, :],
                                     probs[(UNITS * j + n) % PRING][:, i * T:(i + 1) * T], start=True, stop=True)
                last.then_inc(S["pv_unit"], 1)

            def natural(beta):
                pe.wait_ge(S["cU_ok"], beta + 1)
                pe.wait_ge(S["ctxn_ok"], beta)
                four(natbank, lambda w: ctxU[:, w * T:(w + 1) * T]).then_inc(S["nat_ps"], 1)

            def turn_max(sbatch, b):
                pe.wait_ge(S["max_ok"], 4 * (sbatch + 1))
                pe.transpose(nmbank[0:H, 0:T], negmax[b % 2][:, :], ident[:, :]).then_inc(S["nm_ps"], 1)

            def turn_ctx(beta):
                pe.wait_ge(S["ctxn_ok"], beta + 1)
                pe.transpose(mbank[:, 0:T], ctxn[:, :, :].rearrange("p h d -> p (h d)"), ident[:, :])\
                    .then_inc(S["cT2_ps"], 1)

            def project(beta):
                pe.wait_ge(S["cT2_sb"], beta + 1)
                pe.matmul(mbank[:, 0:D], ctxT[:, :], wo_sb[:, :], start=True, stop=True).then_inc(S["proj_ps"], 1)

            def attend(s, sj, t, tj):
                tfirst = t is None or (isinstance(t, int) and t == 0)
                if s is not None:
                    if isinstance(s, int):
                        loads = s // NBUF
                    else:
                        loads = s_loads(s, sj)
                    pe.wait_ge(op_in[sj], 16 * LOADS * (loads + 1))
                if t is not None:
                    pe.wait_ge(S["v_ok"], t + 1)
                for n in range(UNITS):
                    su = s_unit(s, sj, n) if s is not None else None
                    tu = t_unit(t, tj, n) if t is not None else None
                    for i in range(4):
                        if su is not None:
                            ms = next(su)
                        if tu is not None:
                            mt = next(tu)
                    if su is not None:
                        ms.then_inc(S["s_done"], 1)
                    if tu is not None:
                        mt.then_inc(S["t_done"], 1)
                    i, bt = n % 4, (4 * t if t is not None else 0) + n // 4
                    if t is not None:
                        if i == 0 and not (tfirst and n == 0):
                            if n > 0:
                                pv_of(t, tj, n - 1)
                            else:
                                pv_of(t - 1, (tj - 1) % NBUF, UNITS - 1)
                            if not (tfirst and n < 8):
                                project(bt - 2)
                        if i == 1 and not (tfirst and n < 4):
                            natural(bt - 1)
                        if i == 2:
                            pv_of(t, tj, n - 2)
                            pv_of(t, tj, n - 1)
                        if i == 3:
                            pv_of(t, tj, n - 1)
                            if not (tfirst and n < 4):
                                if not (tfirst and n < 8):
                                    pe.wait_ge(S["x1_ok"], bt - 1)
                                turn_ctx(bt - 1)
                    if i == 1:
                        sbatch = (4 * s if s is not None else 4 * NG) + n // 4 - 1
                        if (s is not None or n == 1) and not (isinstance(s, int) and s == 0 and n < 4):
                            if not (isinstance(s, int) and s == 0 and n < 8):
                                pe.wait_ge(S["nm_ok"], sbatch)
                            turn_max(sbatch, (n // 4 - 1) % 4)

            attend(0, 0, None, None)
            attend(1, 1, 0, 0)
            with pe.Fori(0, 2) as r:
                s_loads = lambda s, sj: r + (1 if sj != 2 else 0)
                for j in range(3):
                    attend(3 * r + 2 + j, (2 + j) % NBUF, 3 * r + 1 + j, (1 + j) % NBUF)
            attend(None, None, 7, 1)
            pv_of(7, 1, UNITS - 1)
            project(4 * NG - 2)
            natural(4 * NG - 1)
            pe.wait_ge(S["x1_ok"], 4 * NG - 1)
            turn_ctx(4 * NG - 1)
            project(4 * NG - 1)

            pe.wait_ge(S["max_ok"], UNITS * NG)
            pe.wait_ge(S["exp_ok"], UNITS * NG)
            pe.wait_ge(S["wtap_ok"], CT * TAPS)
            for i in range(TAPS + 1):
                src = (lambda c: wtap[:, c, i, :]) if i < TAPS else (lambda c: w2_n[:, c * 128:(c + 1) * 128])
                four(bank[i], src).then_inc(S["wtr_ps"], 1)
            pe.wait_ge(S["w_sb"], TAPS + 1)

            pe.wait_ge(S["x1_ok"], 4 * NG)
            pe.wait_ge(S["ctxn_ok"], 4 * NG)

            def stage3(f, fu, k, ku):
                def conv(c):
                    if not (isinstance(f, int) and f < 1 and c < 2):
                        pe.wait_ge(S["z_ok"], CT * f + c - 1)
                    for tap in range(TAPS):
                        last = pe.matmul(ybank[c % 2][:, :], w1t[:, c, tap, :], xqT[:, :, tap:tap + T],
                                         start=(tap == 0), stop=(tap == TAPS - 1))
                    last.then_inc(S["y_ps"], 1)

                if f is not None:
                    pe.wait_ge(S["xq_ok"], f + 1)
                    four(xqbank, lambda b: xn[:, b * 128:(b + 1) * 128]).then_inc(S["xqT_ps"], 1)
                if k is not None:
                    pe.wait_ge(S["z_ok"], CT * (k + 1))
                    for b in range(G):
                        if not (isinstance(k, int) and k < 1 and b < 2):
                            pe.wait_ge(S["zmax_ok"], G * k + b - 1)
                        four(ztbank[b % 2], lambda c: z[ku][:, c, b * T:(b + 1) * T]).then_inc(S["zt_ps"], 1)
                if f is not None:
                    pe.wait_ge(S["xqT_sb"], f + 1)
                    conv(0)
                    conv(1)
                if k is not None:
                    pe.wait_ge(S["diag_ok"], k + 1)
                    for b in range(G):
                        last = pe.matmul(scbank[:, b * T:(b + 1) * T], ones[:, :], diag[:, b, :], start=True, stop=True)
                    last.then_inc(S["sc_ps"], 1)
                if f is not None:
                    conv(2)
                    conv(3)
                if k is not None:
                    pe.wait_ge(S["zi_ok"], k + 1)
                    for b in range(G):
                        for c in range(CT):
                            last = pe.matmul(obank[:, b * D:(b + 1) * D], zi[:, c, b * T:(b + 1) * T], w2t[:, c, :],
                                             start=(c == 0), stop=(c == CT - 1))
                    last.then_inc(S["o_ps"], 1)

            stage3(0, 0, None, None)
            stage3(1, 1, 0, 0)
            with pe.Fori(0, (NG - 2) // 2) as r:
                for u in range(2):
                    stage3(2 * r + 2 + u, u, 2 * r + 1 + u, 1 - u)
            stage3(None, None, NG - 1, 1)


_INS = ["x", "ctx_1024", "L0_xattn_Wq", "L0_xattn_bq", "L0_xattn_Wk", "L0_xattn_bk", "L0_xattn_Wv", "L0_xattn_bv",
        "L0_xattn_Wo", "L0_xattn_bo", "L0_ffn_w1", "L0_ffn_conv_w", "L0_ffn_conv_b", "L0_ffn_w2"]


def kernel(**inputs):
    import numpy as _np
    import concourse.bacc as _bacc
    from concourse import mybir as _mybir
    from concourse.bass_utils import run_bass_kernel_spmd as _run

    nc = _bacc.Bacc("TRN2", target_bir_lowering=False, num_devices=1)
    arrays, args = {}, []
    for name in _INS:
        a = _np.ascontiguousarray(inputs[name])
        arrays[f"in_{name}_dram"] = a
        args.append(nc.dram_tensor(f"in_{name}_dram", a.shape, _mybir.dt.from_np(a.dtype), kind="ExternalInput").ap())
    args.append(nc.dram_tensor("out_0_dram", inputs["x"].shape, _mybir.dt.float32, kind="ExternalOutput").ap())
    xattn_ffn_kernel(nc, *args)
    r = _run(nc, [arrays], core_ids=[0])
    return r.results[0]["out_0_dram"]
```

```python
from contextlib import ExitStack

import concourse.bass as bass
from concourse import mybir

F32 = mybir.dt.float32
BF16 = mybir.dt.bfloat16
ALU = mybir.AluOpType
ACT = mybir.ActivationFunctionType
AX = mybir.AxisListType

ROUND = 1.5 * 2.0 ** 23
MASKED = -1.0e30
SMALLEST = 1e-5
EPS = 1e-5


def xattn_ffn_kernel(nc, x, ctx_in, Wq, bq, Wk, bk, Wv, bv, Wo, bo, w1, conv_w, conv_b, w2, out):
    B, T, D = x.shape
    H, DK = 16, 8
    HID = w1.shape[0]
    CT = HID // 128
    TAPS = conv_w.shape[2]
    G = 4
    NG = B // G
    GT = G * T
    GH = G * H
    NSEL = T // 2
    HP = H // 2
    PARTS = 3
    NSIX = 6
    NPROD = NSIX * DK
    KS = 126
    KT = 128
    VW = DK + 1
    UNITS = 16
    NBUF = 3
    SRING, TRING, PRING = 2, 2, 4
    SCALE = float(DK) ** -0.5
    STORE = 16 * PARTS
    NSETS = NG // 2
    LOADS = 6

    scr_q = nc.dram_tensor("scr_q", (NG, NSIX, D, GT), BF16).ap()
    scr_k = nc.dram_tensor("scr_k", (NG, NSIX, D, GT), BF16).ap()
    scr_m = nc.dram_tensor("scr_m", (NSETS, 2 * GH, T), BF16).ap()

    ctx_g = ctx_in.rearrange("(g b) t d -> g t b d", b=G)
    out_g = out.rearrange("(g b) t d -> g t b d", b=G)

    with ExitStack() as ctx:
        def sb(name, shape, dt):
            return ctx.enter_context(nc.sbuf_tensor(name, shape, dt))

        def sem(name):
            return ctx.enter_context(nc.semaphore(name))

        bank = [ctx.enter_context(nc.psum_tensor(f"bank{i}", [128, 512], F32)) for i in range(8)]

        ident = sb("ident", [128, 128], F32)
        ones = sb("ones", [128, 128], F32)
        minus_half = sb("minus_half", [128, G], F32)
        wq_sb = sb("wq_sb", [D, D], F32)
        wk_sb = sb("wk_sb", [D, D], F32)
        wqp = sb("wqp", [D, D], F32)
        wkp = sb("wkp", [D, D], F32)
        wv_sb = sb("wv_sb", [D, D], F32)
        wo_sb = sb("wo_sb", [D, D], F32)
        bq_c = sb("bq_c", [D, 1], F32)
        bk_c = sb("bk_c", [D, 1], F32)
        bv_r = sb("bv_r", [128, D], F32)
        bo_r = sb("bo_r", [128, D], F32)
        w1_n = sb("w1_n", [128, CT, D], F32)
        w2_n = sb("w2_n", [128, HID], F32)
        cw = sb("cw", [128, CT, TAPS], F32)
        cb = sb("cb", [128, CT], F32)
        wabs = sb("wabs", [128, 2], F32)
        wsc = sb("wsc", [128, 2], F32)
        winv = sb("winv", [128, 2], F32)
        x_all = sb("x_all", [128, B * D], F32)
        mask_all = sb("mask_all", [128, B * H], F32)

        qop = [[sb(f"qop{i}_{h}", [128, HP, GT], BF16) for h in range(2)] for i in range(NBUF)]
        kop = [sb(f"kop{i}", [128, HP, GT], BF16) for i in range(NBUF)]
        vop = [sb(f"vop{i}", [128, GH, VW], F32) for i in range(NBUF)]
        negmax = [sb(f"negmax{i}", [128, H], F32) for i in range(2)]
        nmT = [sb(f"nmT{i}", [H, 2, 2 * T], BF16) for i in range(2)]
        probs = [sb(f"probs{i}", [128, 512], F32) for i in range(PRING)]
        ctxU = sb("ctxU", [128, 512], F32)
        rden = sb("rden", [128, H], F32)
        rmask = sb("rmask", [128, H], F32)
        ctxn = sb("ctxn", [128, H, DK], F32)
        ctxT = sb("ctxT", [128, T], F32)
        v_all = sb("v_all", [128, NG * GH * VW], F32)
        w2t = sb("w2t", [128, CT, D], BF16)
        w1t = sb("w1t", [D, CT, TAPS, 128], F32)
        wtmp = sb("wtmp", [128, 512], F32)
        wtap = sb("wtap", [128, CT, TAPS, D], F32)

        stats = sb("stats", [128, G, 6], F32)
        mv = sb("mv", [128, G, 2], F32)
        vare = sb("vare", [128, G], F32)
        rstd = sb("rstd", [128, G], F32)
        xn = sb("xn", [128, GT], F32)

        whole, ctx = ctx, ExitStack()
        ctx_sb = [sb(f"ctx_sb{i}", [128, GT], F32) for i in range(2)]
        xT = sb("xT", [128, GT], F32)
        cT = sb("cT", [128, GT], F32)
        q32 = sb("q32", [128, GT], F32)
        k32 = sb("k32", [128, GT], F32)
        qr = sb("qr", [128, GT], F32)
        kr = sb("kr", [128, GT], F32)
        qp = [sb(f"qp{i}", [128, PARTS, GT], BF16) for i in range(2)]
        kp = [sb(f"kp{i}", [128, PARTS, GT], BF16) for i in range(2)]
        sq = sb("sq", [128, GT], F32)
        norm_all = sb("norm_all", [128, B * H], F32)
        work = sb("work", [128, NSETS, T], F32)
        top8 = sb("top8", [128, NSETS, 8], F32)
        maskT = sb("maskT", [128, NSETS, T], F32)
        negmask = sb("negmask", [128, NSETS, T], BF16)
        ctx.close()
        ctx = whole

        xn2 = sb("xn2", [128, G, D], F32)
        xr = sb("xr", [128, G, D], F32)
        amax = sb("amax", [128, G], F32)
        amaxc = sb("amaxc", [128, G], F32)
        arec = sb("arec", [128, G], F32)
        asc = sb("asc", [128, G], F32)
        ainv = sb("ainv", [128, G], F32)
        xqT = sb("xqT", [128, G, T + 2], F32)
        z = [sb(f"z{i}", [128, CT, GT], F32) for i in range(2)]
        zs = sb("zs", [128, CT, GT], F32)
        zi = sb("zi", [128, CT, GT], BF16)
        zmax = sb("zmax", [128, G], F32)
        zmaxc = sb("zmaxc", [128, G], F32)
        zrec = sb("zrec", [128, G], F32)
        zsc = sb("zsc", [128, G], F32)
        zinv = sb("zinv", [128, G], F32)
        zout = sb("zout", [128, G], F32)
        diag = sb("diag", [128, G, 128], F32)
        scb = sb("scb", [128, GT], F32)
        osb = sb("osb", [128, GT], F32)

        names = """k_step ones_in ones2_in x1_in xr_in v_ok ops_free spare wp_ok
            const_p const_q w_in w2_in const_z const_i const_v w_step wabs_ps t_step wtap_ok wtr_ps w_sb
            x_in st_m
            stat_step var_ok rstd_ok xn_ok xT_ps cT_ps xT_sb cT_sb q_ps k_ps v_ps q32_ok qhi_ok k32_ok khi_ok
            n_ps sq_ok norm_ok nT_ps top_step maskT_ok negm_ok m_ps mask_ok v_sb
            qr_ok kr_ok qmid_ok kmid_ok qlo_ok klo_ok xbo_ok
            s_done max_ok t_done exp_ok pv_unit cU_ok nat_ps att_step ctxn_ok cT2_ps cT2_sb proj_ps x1_ok
            nm_ps nm_hi nm_ok
            stat3 var3 rstd3 f_step xq_ok xqT_ps xqT_sb y_ps z_ok zt_ps zmax_ok diag_ok sc_ps scb_ok
            zs_ok zsl_ok zi_ok o_ps o_ok out_st""".split()
        S = {n: sem(n) for n in names}
        op_in = [sem(f"op_in{i}") for i in range(NBUF)]
        st = {f: [sem(f"st_{f}{i}") for i in range(2)] for f in "qk"}
        ctx_s = [sem(f"ctx_s{i}") for i in range(2)]
        nm_in = [sem(f"nm_in{i}") for i in range(2)]

        def apart(eng, s, n):
            eng.wait_ge(s, n)
            eng.sem_inc(S["spare"], 1)

        block = ctx.enter_context(nc.Block())
        psX, psC, psQ, psK, psV, psN, psM, psW = bank
        sbank, tbank, nmbank, pvbank, natbank, mbank = bank[0:2], bank[2:4], bank[4], bank[5], bank[6], bank[7]
        ybank, ztbank, scbank, obank, xqbank = bank[0:2], bank[2:4], bank[4], bank[5], bank[6]

        @block.sync
        def _(sp):
            def load_x(g, n, inc):
                sp.dma_start(x_all[:, g * GT:(g + n) * GT].rearrange("p (b d) -> p b d", d=D),
                             x.rearrange("b t d -> t b d")[:, g * G:(g + n) * G]).then_inc(S[inc], 16)

            def load_ctx(g, buf):
                sp.dma_start(ctx_sb[buf][:, :].rearrange("p (b d) -> p b d", b=G), ctx_g[g]).then_inc(ctx_s[buf], 16)

            load_x(0, 1, "x_in")
            load_ctx(0, 0)
            for dst, src in ((wq_sb, Wq), (wk_sb, Wk), (wv_sb, Wv)):
                sp.dma_start(dst[:, :], src).then_inc(S["w_in"], 16)
            for dst, src in ((bq_c, bq), (bk_c, bk)):
                for h in range(2):
                    sp.dma_start(dst[64 * h:64 * h + 64, :],
                                 src.rearrange("(h k d a) -> h d k a", h=2, d=DK, a=1)[h],
                                 allow_slow_non_contiguous=True).then_inc(S["w_in"], 16)
            sp.dma_start(bv_r[:, :], bv.partition_broadcast(128)).then_inc(S["w_in"], 16)
            sp.dma_start(bo_r[:, :], bo.partition_broadcast(128)).then_inc(S["w_in"], 16)
            load_x(1, 1, "x1_in")
            load_ctx(1, 1)
            load_x(2, NG - 2, "xr_in")
            sp.dma_start(w1_n[:, :, :], w1.rearrange("(c p) d -> p c d", p=128)).then_inc(S["w2_in"], 16)
            sp.dma_start(w2_n[:, :], w2).then_inc(S["w2_in"], 16)
            sp.dma_start(cw[:, :, :], conv_w.rearrange("(c p) a k -> p c (a k)", p=128)).then_inc(S["w2_in"], 16)
            for c in range(CT):
                sp.dma_start(cb[:, c:c + 1], conv_b[c * 128:(c + 1) * 128].rearrange("(p a) -> p a", a=1))\
                    .then_inc(S["w2_in"], 16)
            sp.dma_start(wo_sb[:, :], Wo).then_inc(S["w2_in"], 16)

            def store(g, buf):
                for f, part, scr in (("q", qp, scr_q), ("k", kp, scr_k)):
                    for p in ("hi", "mid", "lo"):
                        sp.wait_ge(S[f + p + "_ok"], g + 1)
                    row = 0
                    for q_part, n in ((0, 3), (1, 2), (2, 1)):
                        if f == "q":
                            src = part[buf][:, q_part:q_part + 1, :].broadcast_to([D, n, GT])
                        else:
                            src = part[buf][:, 0:n, :]
                        sp.dma_start(scr[g][row:row + n].rearrange("a p t -> p a t"), src).then_inc(st[f][buf], 16)
                        row += n

            for f in "qk":
                sp.sem_inc(st[f][0], STORE)
                sp.sem_inc(st[f][1], STORE)
            with sp.Fori(0, (NG - 2) // 2) as r:
                for u in range(2):
                    g = 2 * r + 1 + u
                    sp.wait_ge(S["cT_ps"], g)
                    load_ctx(g + 1, u)
                    store(g - 1, u)
            store(NG - 2, 0)
            store(NG - 1, 1)
            def load_ops(g, buf):
                for f in "qk":
                    for u in ((g,) if isinstance(g, int) and g < 2 else (0, 1)):
                        sp.wait_ge(st[f][u], 2 * STORE if isinstance(g, int) and g < 2 else STORE * (NG // 2 + 1))
                inc = op_in[buf]
                for half in range(2):
                    p0 = 64 * half
                    for dst, scr in ((qop[buf][half], scr_q), (kop[buf], scr_k)):
                        sp.dma_start(dst[p0:p0 + NPROD, :, :].rearrange("p k t -> p (k t)"),
                                     scr[g].rearrange("s (h d k) t -> h s d (k t)", h=2, d=DK)[half]).then_inc(inc, 16)
                if isinstance(g, int) and g == 0:
                    sp.wait_ge(S["negm_ok"], 1)
                    sp.dma_start(scr_m.rearrange("m p t -> p m t"), negmask[:, :, :]).then_inc(S["st_m"], 16)
                    sp.wait_ge(S["st_m"], 16)
                for half in range(2):
                    p0 = 64 * half
                    sp.dma_start(kop[buf][p0 + NPROD:p0 + NPROD + 1, :, :].rearrange("p k (b t) -> p k b t", b=G),
                                 scr_m.rearrange("m (e b h k) t -> (m e) h k b t", e=2, b=G, h=2)[g][half:half + 1])\
                        .then_inc(inc, 16)

            def move_max(s, pair, buf):
                sp.wait_ge(S["nm_ok"], 4 * s + 2 * pair + 2)
                for half in range(2):
                    for part in range(2):
                        row = KS + part
                        sp.dma_start(qop[buf][half][row:row + 1, :, 2 * pair * T:2 * (pair + 1) * T],
                                     nmT[pair][HP * half:HP * half + HP, part, :]).then_inc(nm_in[pair], 16)

            def row_of_ones(i, inc):
                for half in range(2):
                    row = 64 * half + NPROD
                    sp.dma_start(qop[i][half][row:row + 1, :, :].rearrange("p k t -> p (k t)"),
                                 kop[2][0:1, :, :].rearrange("p k t -> p (k t)")).then_inc(S[inc], 16)
            sp.wait_ge(S["const_p"], 2 * 2 + NBUF)
            row_of_ones(0, "ones_in")
            row_of_ones(1, "ones_in")
            load_ops(0, 0)
            load_ops(1, 1)
            sp.wait_ge(S["const_q"], 2)
            row_of_ones(2, "ones2_in")
            move_max(0, 0, 0)
            sp.wait_ge(S["ones2_in"], 32)
            sp.sem_inc(S["ops_free"], 1)
            with sp.Fori(0, 2) as r:
                for j in range(NBUF):
                    s = 3 * r + 2 + j
                    move_max(s - 2, 1, j % NBUF)
                    sp.wait_ge(S["ops_free"], s - 1)
                    load_ops(s, (2 + j) % NBUF)
                    move_max(s - 1, 0, (1 + j) % NBUF)
            move_max(6, 1, 0)
            move_max(7, 0, 1)
            move_max(7, 1, 1)

            def store_out(g):
                sp.wait_ge(S["o_ok"], g + 1)
                sp.dma_start(out_g[g], osb[:, :].rearrange("p (b d) -> p b d", b=G)).then_inc(S["out_st"], 16)
            with sp.Fori(0, NG) as g:
                store_out(g)
            sp.wait_ge(S["out_st"], 16 * NG)

        @block.gpsimd
        def _(pool):
            pool.memset(ident[:, :], 0.0).then_inc(S["const_z"], 1)
            pool.wait_ge(S["const_z"], 1)
            pool.affine_select(out=ident[:, :], in_=ident[:, :], compare_op=ALU.not_equal, fill=1.0, base=0,
                               pattern=[[-1, 128]], channel_multiplier=1).then_inc(S["const_i"], 1)
            pool.memset(minus_half[:, :], -0.5).then_inc(S["const_z"], 1)
            pool.wait_ge(S["const_z"], 2)
            def inv_std(ok_in, ok_out, n):
                pool.wait_ge(ok_in, n)
                pool.tensor_tensor(rstd[:, :], vare[:, :], minus_half[:, :], ALU.pow).then_inc(ok_out, 1)

            def rest(g, u):
                for f, part, r, t in (("q", qp, qr, q32), ("k", kp, kr, k32)):
                    pool.wait_ge(S[f + "hi_ok"], g + 1)
                    pool.wait_ge(S[f + "32_ok"], g + 1)
                    if not (isinstance(g, int) and g < 1):
                        pool.wait_ge(S[f + "lo_ok"], g)
                    pool.tensor_tensor(r[:, :], t[:, :], part[u][:, 0, :], ALU.subtract).then_inc(S[f + "r_ok"], 1)

            def low(g, u):
                for f, part, r in (("q", qp, qr), ("k", kp, kr)):
                    pool.wait_ge(S[f + "mid_ok"], g + 1)
                    pool.tensor_tensor(part[u][:, 2, :], r[:, :], part[u][:, 1, :], ALU.subtract).then_inc(S[f + "lo_ok"], 1)

            def stage1(g, u, more):
                if more:
                    inv_std(S["var_ok"], S["rstd_ok"], g + 2)
                if not (isinstance(g, int) and g < 1):
                    low(g - 1, 1 - u)
                rest(g, u)

            inv_std(S["var_ok"], S["rstd_ok"], 1)
            pool.wait_ge(S["w_in"], 16 * 9)
            stage1(0, 0, True)
            for k in kop:
                pool.memset(k[:, :, :].rearrange("p k t -> p (k t)"), 1.0).then_inc(S["const_p"], 1)
            with pool.Fori(0, (NG - 2) // 2) as r:
                for u in range(2):
                    stage1(2 * r + 1 + u, 1 - u, True)
            stage1(NG - 1, 1, False)
            low(NG - 1, 1)
            for q in qop[2]:
                pool.memset(q[:, :, :].rearrange("p k t -> p (k t)"), 0.0).then_inc(S["const_q"], 1)
            pool.wait_ge(S["xn_ok"], NG)
            xb = x_all[:, :].rearrange("p (b d) -> p b d", b=B)
            pool.tensor_tensor(xb, xb, bo_r[:, :].unsqueeze(1).broadcast_to([128, B, D]), ALU.add).then_inc(S["xbo_ok"], 1)

            pool.wait_ge(S["w_step"], 5)
            tstep = [0]

            def chain(ins):
                tstep[0] += 1
                ins.then_inc(S["t_step"], 1)
                pool.wait_ge(S["t_step"], tstep[0])

            w1f = w1_n[:, :, :].rearrange("p c d -> p (c d)")
            for wf, k in ((w1f, 0), (w2_n[:, :], 1)):
                chain(pool.tensor_scalar(wtmp[:, :], wf, wsc[:, k:k + 1], ROUND, ALU.mult, ALU.add))
                chain(pool.tensor_scalar(wtmp[:, :], wtmp[:, :], ROUND, 1.0, ALU.subtract, ALU.min))
                chain(pool.tensor_scalar(wf, wtmp[:, :], -1.0, None, ALU.max))
            chain(pool.tensor_scalar(w1f, w1f, winv[:, 0:1], None, ALU.mult))
            for c in range(CT):
                for k in range(TAPS):
                    pool.tensor_scalar(wtap[:, c, k, :], w1_n[:, c, :], cw[:, c, k:k + 1], None, ALU.mult)\
                        .then_inc(S["wtap_ok"], 1)

            def scaled(k, u):
                pool.wait_ge(S["scb_ok"], k + 1)
                if not (isinstance(k, int) and k < 1):
                    pool.wait_ge(S["zi_ok"], k)
                for c in range(CT - 1):
                    pool.tensor_tensor(zs[:, c, :], z[u][:, c, :], scb[:, :], ALU.mult).then_inc(S["zs_ok"], 1)

            inv_std(S["var3"], S["rstd3"], 1)
            inv_std(S["var3"], S["rstd3"], 2)
            inv_std(S["var3"], S["rstd3"], 3)
            scaled(0, 0)
            with pool.Fori(0, (NG - 4) // 2) as r:
                for u in range(2):
                    inv_std(S["var3"], S["rstd3"], 2 * r + u + 4)
                    scaled(2 * r + 1 + u, 1 - u)
            inv_std(S["var3"], S["rstd3"], NG)
            scaled(NG - 3, 1)
            scaled(NG - 2, 0)
            scaled(NG - 1, 1)

        @block.scalar
        def _(act):
            act.wait_ge(S["w_in"], 16 * 9)

            def parts(g, u, turn, f, ps, t32, part, bias):
                act.wait_ge(S[f + "_ps"], g + 1)
                if not (isinstance(g, int) and g < 1):
                    act.wait_ge(S[f + "r_ok"], g)
                    act.wait_ge(S["n_ps"], g)
                    act.wait_ge(st[f][u], STORE * turn)
                act.activation(t32[:, :], ps[:, :], ACT.Identity, bias=bias[:, 0:1]).then_inc(S[f + "32_ok"], 1)
                act.activation(part[u][:, 0, :], ps[:, :], ACT.Identity, bias=bias[:, 0:1]).then_inc(S[f + "hi_ok"], 1)

            def squares(g):
                act.wait_ge(S["n_ps"], g + 1)
                act.wait_ge(S["norm_ok"], g + 1)
                act.activation(sq[:, :], psN[:, :], ACT.Square).then_inc(S["sq_ok"], 1)

            def middle(g, u):
                for f, part, r in (("q", qp, qr), ("k", kp, kr)):
                    act.wait_ge(S[f + "r_ok"], g + 1)
                    act.activation(part[u][:, 1, :], r[:, :], ACT.Copy).then_inc(S[f + "mid_ok"], 1)

            def stage1(g, u, turn):
                act.wait_ge(S["xT_ps"], g + 1)
                act.activation(xT[:, :], psX[:, :], ACT.Copy).then_inc(S["xT_sb"], 1)
                act.wait_ge(S["cT_ps"], g + 1)
                if not (isinstance(g, int) and g < 1):
                    act.wait_ge(S["v_ps"], g)
                act.activation(cT[:, :], psC[:, :], ACT.Copy).then_inc(S["cT_sb"], 1)
                if not (isinstance(g, int) and g < 1):
                    middle(g - 1, 1 - u)
                    squares(g - 1)
                parts(g, u, turn, "q", psQ, q32, qp, bq_c)
                parts(g, u, turn, "k", psK, k32, kp, bk_c)

            stage1(0, 0, 1)
            with act.Fori(0, (NG - 2) // 2) as r:
                stage1(2 * r + 1, 1, r + 1)
                stage1(2 * r + 2, 0, r + 2)
            stage1(NG - 1, 1, NG // 2)
            middle(NG - 1, 1)
            squares(NG - 1)

            def attend(t, j, beside={}):
                first = isinstance(t, int) and t == 0
                act.activation(vop[j][:, :, :].rearrange("p h c -> p (h c)"),
                               v_all[:, bass.ds(t * (GH * VW), GH * VW)], ACT.Copy).then_inc(S["v_ok"], 1)
                for n in range(UNITS):
                    N = UNITS * t + n
                    act.wait_ge(S["t_done"], N + 1)
                    if not (first and n < PRING):
                        act.wait_ge(S["pv_unit"], N - PRING + 1)
                    act.activation(probs[(UNITS * j + n) % PRING][:, :], tbank[n % TRING][:, :], ACT.Exp,
                                   scale=SCALE).then_inc(S["exp_ok"], 1)
                    beta = 4 * t + n // 4 - 1
                    if not (first and n < 4):
                        if n % 4 == 0:
                            context(beta)
                        if n == 0:
                            act.sem_inc(S["ops_free"], 1)
                    if n % 4 == 1 and not (first and n < 8):
                        turned(beta - 1)
                    if n in beside:
                        beside[n]()

            def context(beta):
                act.wait_ge(S["pv_unit"], 4 * (beta + 1))
                act.wait_ge(S["nat_ps"], beta)
                act.activation(ctxU[:, :], pvbank[:, :], ACT.Copy).then_inc(S["cU_ok"], 1)

            def turned(beta):
                act.wait_ge(S["cT2_ps"], beta + 1)
                act.wait_ge(S["proj_ps"], beta)
                act.activation(ctxT[:, :], mbank[:, 0:T], ACT.Copy).then_inc(S["cT2_sb"], 1)

            act.wait_ge(S["v_sb"], NG)
            attend(0, 0)
            with act.Fori(0, 2) as r:
                for j in range(3):
                    attend(3 * r + 1 + j, (1 + j) % NBUF)

            def weights(i):
                act.wait_ge(S["wtr_ps"], i + 1)
                dst = w1t[:, :, i, :] if i < TAPS else w2t[:, :, :]
                act.activation(dst, bank[i % 2][:, :].rearrange("p (c k) -> p c k", c=CT), ACT.Copy).then_inc(S["w_sb"], 1)

            attend(7, 1, {0: lambda: weights(0), 1: lambda: weights(1), 4: lambda: weights(2), 5: lambda: weights(3)})
            context(4 * NG - 1)
            turned(4 * NG - 2)
            turned(4 * NG - 1)

            def stage3(f, fu, k):
                def silu(c):
                    act.wait_ge(S["y_ps"], CT * f + c + 1)
                    if c == 0 and not (isinstance(f, int) and f < 2):
                        act.wait_ge(S["zs_ok"], (CT - 1) * (f - 1))
                        act.wait_ge(S["zsl_ok"], f - 1)
                    act.activation(z[fu][:, c, :], ybank[c % 2][:, :], ACT.Silu, bias=cb[:, c:c + 1]).then_inc(S["z_ok"], 1)

                if f is not None:
                    act.wait_ge(S["xqT_ps"], f + 1)
                    if not (isinstance(f, int) and f < 1):
                        act.wait_ge(S["y_ps"], CT * f)
                    act.activation(xqT[:, :, 1:T + 1], xqbank[:, :].rearrange("p (b t) -> p b t", b=G),
                                   ACT.Copy).then_inc(S["xqT_sb"], 1)
                    silu(0)
                    silu(1)
                if k is not None:
                    act.wait_ge(S["sc_ps"], k + 1)
                    if not (isinstance(k, int) and k < 1):
                        act.wait_ge(S["zs_ok"], (CT - 1) * k)
                        act.wait_ge(S["zsl_ok"], k)
                    act.activation(scb[:, :], scbank[:, :], ACT.Copy).then_inc(S["scb_ok"], 1)
                if f is not None:
                    silu(2)
                    silu(3)

            act.wait_ge(S["w2_in"], 16 * (4 + CT))
            stage3(0, 0, None)
            stage3(1, 1, 0)
            with act.Fori(0, (NG - 2) // 2) as r:
                for u in range(2):
                    stage3(2 * r + 2 + u, u, 2 * r + 1 + u)
            stage3(None, None, NG - 1)

        @block.vector
        def _(dve):
            dve.sem_inc(S["norm_ok"], 1)
            dve.sem_inc(S["sq_ok"], 1)
            dve.memset(ones[:, :], 1.0).then_inc(S["const_v"], 1)
            dve.memset(v_all[:, :].rearrange("p (h c) -> p h c", c=VW)[:, :, DK:VW], 1.0).then_inc(S["const_v"], 1)

            def clear(q):
                dve.memset(q[:, :, :].rearrange("p k t -> p (k t)"), 0.0).then_inc(S["const_p"], 1)
            clear(qop[0][0])

            def stats_of(g, step, ok, count):
                for b in range(G):
                    dve.bn_stats(stats[:, b, :], x_all[:, bass.ds(g * GT + b * D, D)]).then_inc(step, 1)
                apart(dve, step, count * 2 * G + G)
                for b in range(G):
                    dve.bn_aggr(mv[:, b, :], stats[:, b, :]).then_inc(step, 1)
                dve.wait_ge(step, (count + 1) * 2 * G)
                dve.tensor_scalar(vare[:, :], mv[:, :, 1], EPS, None, ALU.add).then_inc(ok, 1)

            def normalise(g, dst):
                for b in range(G):
                    last = dve.tensor_scalar(dst[:, b * D:(b + 1) * D], x_all[:, bass.ds(g * GT + b * D, D)],
                                             mv[:, b, 0:1], rstd[:, b:b + 1], ALU.subtract, ALU.mult)
                return last

            def select():
                step = S["top_step"]
                dve.wait_ge(S["nT_ps"], NSETS)
                dve.tensor_copy(work[:, :, :].rearrange("p m t -> p (m t)"), psM[:, :]).then_inc(step, 1)
                for i in range(NSEL // 8):
                    for m in range(NSETS):
                        dve.wait_ge(step, 1 if i == 0 else 2 + 2 * NSETS * i - NSETS + m)
                        dve.max(top8[:, m, :], work[:, m, :]).then_inc(step, 1)
                    for m in range(NSETS):
                        dve.wait_ge(step, 2 + 2 * NSETS * i + m)
                        dve.match_replace(work[:, m, :], top8[:, m, :], work[:, m, :], -1.0).then_inc(step, 1)
                dve.wait_ge(step, 1 + 2 * NSETS * (NSEL // 8))
                dve.tensor_scalar(negmask[:, :, :], work[:, :, :], 0.0, MASKED, ALU.is_ge, ALU.mult).then_inc(S["negm_ok"], 1)
                dve.tensor_scalar(maskT[:, :, :], work[:, :, :], 0.0, None, ALU.is_lt).then_inc(S["maskT_ok"], 1)
                dve.wait_ge(S["m_ps"], NSETS)
                dve.tensor_copy(mask_all[:, :], psW[:, :]).then_inc(S["mask_ok"], 1)

            def values(g):
                dve.wait_ge(S["v_ps"], g + 1)
                dve.tensor_tensor(v_all[:, bass.ds(g * (GH * VW), GH * VW)].rearrange("p (b h c) -> p b h c", b=G, c=VW)[:, :, :, 0:DK],
                                  psV[:, :].rearrange("p (b h c) -> p b h c", b=G, c=DK),
                                  bv_r[:, :].rearrange("p (h c) -> p h c", c=DK).unsqueeze(1).broadcast_to([128, G, H, DK]),
                                  ALU.add).then_inc(S["v_sb"], 1)

            def norms(g):
                dve.wait_ge(S["sq_ok"], g + 2)
                dve.tensor_reduce(norm_all[:, bass.ds(g * GH, GH)],
                                  sq[:, :].rearrange("p (h d k) -> p h k d", d=DK, k=HP), AX.X, ALU.add)\
                    .then_inc(S["norm_ok"], 1)

            def stage1(g, x_sem):
                dve.wait_ge(S["rstd_ok"], g + 1)
                if not (isinstance(g, int) and g < 1):
                    dve.wait_ge(S["xT_ps"], g)
                normalise(g, xn).then_inc(S["xn_ok"], 1)
                if not (isinstance(g, int) and g < 1):
                    values(g - 1)
                if x_sem is not None:
                    dve.wait_ge(S[x_sem], 16)
                    dve.wait_ge(S["xn_ok"], g + 1)
                    stats_of(g + 1, S["stat_step"], S["var_ok"], g + 1)
                if not (isinstance(g, int) and g < 1):
                    norms(g - 1)

            dve.wait_ge(S["const_v"], 2)
            dve.wait_ge(S["x_in"], 16)
            stats_of(0, S["stat_step"], S["var_ok"], 0)
            dve.wait_ge(S["w_in"], 16 * 9)
            for dst, src in ((wqp, wq_sb), (wkp, wk_sb)):
                for h in range(2):
                    dve.tensor_copy(dst[:, 64 * h:64 * h + 64].rearrange("p (d k) -> p d k", d=DK),
                                    src[:, 64 * h:64 * h + 64].rearrange("p (k d) -> p d k", d=DK)).then_inc(S["wp_ok"], 1)
            stage1(0, "x1_in")

            for q in (qop[0][1], qop[1][0], qop[1][1]):
                clear(q)

            wstep = [0]

            def chain(ins):
                wstep[0] += 1
                ins.then_inc(S["w_step"], 1)
                dve.wait_ge(S["w_step"], wstep[0])

            dve.wait_ge(S["w2_in"], 16 * (4 + CT))
            chain(dve.tensor_reduce(wabs[:, 0:1], w1_n[:, :, :], AX.XY, ALU.add, apply_absolute_value=True))
            chain(dve.tensor_reduce(wabs[:, 1:2], w2_n[:, :], AX.X, ALU.add, apply_absolute_value=True))
            dve.wait_ge(S["wabs_ps"], 1)
            chain(dve.tensor_scalar(wabs[:, :], psW[:, 0:2], 1.0 / (HID * D), SMALLEST, ALU.mult, ALU.max))
            chain(dve.reciprocal(wsc[:, :], wabs[:, :]))
            chain(dve.reciprocal(winv[:, :], wsc[:, :]))

            with dve.Fori(1, NG - 1) as g:
                stage1(g, "xr_in")
            stage1(NG - 1, None)
            values(NG - 1)
            norms(NG - 1)
            select()

            def maximum(s, j, n):
                N = UNITS * s + n
                dve.wait_ge(S["s_done"], N + 1)
                b, half, q4 = n // 4, n % 2, n % 4 // 2
                if n % 4 == 0 and not (isinstance(s, int) and s == 0 and n < 8):
                    dve.wait_ge(S["nm_ps"], 4 * s + b - 1)
                h0 = HP * half + 4 * q4
                dve.tensor_reduce(negmax[b % 2][:, h0:h0 + 4],
                                  sbank[(UNITS * j + n) % SRING][:, :].rearrange("p (h k) -> p h k", h=4),
                                  AX.X, ALU.max, negate=True).then_inc(S["max_ok"], 1)

            def split_high(sb_index, b):
                dve.wait_ge(S["nm_ps"], sb_index + 1)
                dve.tensor_copy(nmT[b // 2][:, 0, b % 2 * T:(b % 2 + 1) * T], nmbank[0:H, 0:T]).then_inc(S["nm_hi"], 1)

            def split_low(sb_index, b):
                dve.wait_ge(S["nm_hi"], sb_index + 1)
                c = slice(b % 2 * T, (b % 2 + 1) * T)
                dve.tensor_tensor(nmT[b // 2][:, 1, c], nmbank[0:H, 0:T], nmT[b // 2][:, 0, c],
                                  ALU.subtract).then_inc(S["nm_ok"], 1)

            nat = natbank[:, :].rearrange("p (h r) -> p h r", r=32)

            def weigh_rden(beta):
                dve.wait_ge(S["nat_ps"], beta + 1)
                dve.reciprocal(rden[:, :], nat[:, :, DK]).then_inc(S["att_step"], 1)

            def weigh_mask(beta):
                dve.wait_ge(S["att_step"], 2 * beta + 1)
                dve.tensor_tensor(rmask[:, :], rden[:, :], mask_all[:, bass.ds(beta * H, H)], ALU.mult)\
                    .then_inc(S["att_step"], 1)

            def weigh(beta):
                dve.wait_ge(S["att_step"], 2 * beta + 2)
                dve.wait_ge(S["cT2_ps"], beta)
                dve.tensor_tensor(ctxn[:, :, :], nat[:, :, 0:DK], rmask[:, :].unsqueeze(2).broadcast_to([128, H, DK]),
                                  ALU.mult).then_inc(S["ctxn_ok"], 1)

            def residual(beta):
                dve.wait_ge(S["proj_ps"], beta + 1)
                xb = x_all[:, bass.ds(beta * D, D)]
                dve.tensor_tensor(xb, mbank[:, 0:D], xb, ALU.add).then_inc(S["x1_ok"], 1)

            def attend(s, sj, t, beside={}):
                for n in range(UNITS):
                    i = n % 4
                    bt = (4 * t if t is not None else 0) + n // 4
                    late = t is not None and not (isinstance(t, int) and t == 0 and n < 4)
                    later = t is not None and not (isinstance(t, int) and t == 0 and n < 8)
                    latest = t is not None and not (isinstance(t, int) and t == 0 and n < 12)
                    if i == 0 and later:
                        weigh(bt - 2)
                    if i == 3 and late:
                        weigh_rden(bt - 1)
                    if s is not None:
                        maximum(s, sj, n)
                    if i == 0 and latest:
                        residual(bt - 3)
                    if i == 3 and late:
                        weigh_mask(bt - 1)
                    if n in beside:
                        beside[n]()
                    if i >= 2:
                        sbatch = (4 * s if s is not None else 4 * NG) + n // 4 - 1
                        b = (n // 4 - 1) % 4
                        if (s is not None or n < 4) and not (isinstance(s, int) and s == 0 and n < 4):
                            if i == 2:
                                moved = (s if s is not None else NG) - (1 if n < 4 else 0)
                                if not (isinstance(moved, int) and moved < 1):
                                    dve.wait_ge(nm_in[b // 2], 64 * moved)
                                split_high(sbatch, b)
                            else:
                                split_low(sbatch, b)

            NA = 6 + G

            def f(g, n):
                dve.wait_ge(S["f_step"], NA * g + n)

            def stats3(g):
                stats_of(g, S["stat3"], S["var3"], g)

            def magnitudes(g):
                dve.wait_ge(S["rstd3"], g + 1)
                normalise(g, xn2[:, :, :].rearrange("p b d -> p (b d)")).then_inc(S["f_step"], 1)
                f(g, 1)
                dve.tensor_reduce(amax[:, :], xn2[:, :, :], AX.X, ALU.max, apply_absolute_value=True).then_inc(S["f_step"], 1)

            def token_scales(g):
                f(g, 2)
                dve.tensor_scalar(amaxc[:, :], amax[:, :], SMALLEST, None, ALU.max).then_inc(S["f_step"], 1)
                f(g, 3)
                dve.reciprocal(arec[:, :], amaxc[:, :]).then_inc(S["f_step"], 1)
                f(g, 4)
                dve.tensor_scalar(asc[:, :], arec[:, :], 127.0, None, ALU.mult).then_inc(S["f_step"], 1)
                f(g, 5)
                dve.reciprocal(ainv[:, :], asc[:, :]).then_inc(S["f_step"], 1)

            def quantise(g):
                for b in range(G):
                    dve.tensor_scalar(xr[:, b, :], xn2[:, b, :], asc[:, b:b + 1], ROUND, ALU.mult, ALU.add)\
                        .then_inc(S["f_step"], 1)
                f(g, NA)
                if not (isinstance(g, int) and g < 1):
                    dve.wait_ge(S["xqT_ps"], g)
                for b in range(G):
                    last = dve.tensor_scalar(xn[:, b * D:(b + 1) * D], xr[:, b, :], ROUND, ainv[:, b:b + 1],
                                             ALU.subtract, ALU.mult)
                last.then_inc(S["xq_ok"], 1)

            NK = 5

            def largest(k, b):
                dve.wait_ge(S["zt_ps"], G * k + b + 1)
                dve.tensor_reduce(zmax[:, b:b + 1], ztbank[b % 2][:, :], AX.X, ALU.max, apply_absolute_value=True)\
                    .then_inc(S["zmax_ok"], 1)

            def scales(k):
                dve.wait_ge(S["zmax_ok"], G * (k + 1))
                dve.tensor_scalar(zmaxc[:, :], zmax[:, :], SMALLEST, None, ALU.max).then_inc(S["k_step"], 1)
                dve.wait_ge(S["k_step"], NK * k + 1)
                dve.reciprocal(zrec[:, :], zmaxc[:, :]).then_inc(S["k_step"], 1)
                dve.wait_ge(S["k_step"], NK * k + 2)
                dve.tensor_scalar(zsc[:, :], zrec[:, :], 127.0, None, ALU.mult).then_inc(S["k_step"], 1)
                dve.wait_ge(S["k_step"], NK * k + 3)
                for b in range(G):
                    last = dve.tensor_scalar(diag[:, b, :], ident[:, :], zsc[:, b:b + 1], None, ALU.mult)
                last.then_inc(S["diag_ok"], 1)
                dve.reciprocal(zinv[:, :], zsc[:, :]).then_inc(S["k_step"], 1)
                dve.wait_ge(S["k_step"], NK * k + 4)
                dve.tensor_scalar(zout[:, :], zinv[:, :], winv[:, 1:2], None, ALU.mult).then_inc(S["k_step"], 1)

            def last_tile(k, ku):
                dve.wait_ge(S["scb_ok"], k + 1)
                if not (isinstance(k, int) and k < 1):
                    dve.wait_ge(S["zi_ok"], k)
                dve.tensor_tensor(zs[:, CT - 1, :], z[ku][:, CT - 1, :], scb[:, :], ALU.mult).then_inc(S["zsl_ok"], 1)

            def rounded(k):
                if not (isinstance(k, int) and k < 1):
                    dve.wait_ge(S["o_ps"], k)
                for c in range(CT):
                    if c < CT - 1:
                        dve.wait_ge(S["zs_ok"], (CT - 1) * k + c + 1)
                    else:
                        dve.wait_ge(S["zsl_ok"], k + 1)
                    last = dve.tensor_scalar(zi[:, c, :], zs[:, c, :], ROUND, ROUND, ALU.add, ALU.subtract)
                last.then_inc(S["zi_ok"], 1)

            def result(k):
                dve.wait_ge(S["o_ps"], k + 1)
                dve.wait_ge(S["k_step"], NK * (k + 1))
                if not (isinstance(k, int) and k < 1):
                    dve.wait_ge(S["out_st"], 16 * k)
                for b in range(G):
                    last = dve.scalar_tensor_tensor(out=osb[:, b * D:(b + 1) * D], in0=obank[:, b * D:(b + 1) * D],
                                                    scalar=zout[:, b:b + 1], in1=x_all[:, bass.ds(k * GT + b * D, D)],
                                                    op0=ALU.mult, op1=ALU.add)
                last.then_inc(S["o_ok"], 1)

            def stage3(a, k, ku):
                largest(k, 0)
                largest(k, 1)
                if a is not None:
                    stats3(a)
                largest(k, 2)
                largest(k, 3)
                scales(k)
                if a is not None:
                    magnitudes(a)
                    token_scales(a)
                last_tile(k, ku)
                if a is not None:
                    quantise(a)
                rounded(k)
                result(k)

            dve.memset(pvbank[:, :], 0.0).then_inc(S["const_v"], 1)
            dve.wait_ge(S["xbo_ok"], 1)
            attend(0, 0, None)
            attend(1, 1, 0)
            with dve.Fori(0, 2) as r:
                for j in range(3):
                    attend(3 * r + 2 + j, (2 + j) % NBUF, 3 * r + 1 + j)
            dve.wait_ge(S["x1_ok"], 2 * G)
            dve.memset(xqT[:, :, :], 0.0).then_inc(S["const_v"], 1)
            attend(None, None, 7, {1: lambda: stats3(0), 5: lambda: magnitudes(0), 7: lambda: token_scales(0),
                                   9: lambda: quantise(0), 11: lambda: stats3(1), 13: lambda: magnitudes(1),
                                   15: lambda: token_scales(1)})
            residual(4 * NG - 3)
            weigh(4 * NG - 2)
            residual(4 * NG - 2)
            weigh_rden(4 * NG - 1)
            weigh_mask(4 * NG - 1)
            weigh(4 * NG - 1)
            residual(4 * NG - 1)

            dve.wait_ge(S["x1_ok"], B)
            quantise(1)
            stage3(2, 0, 0)
            with dve.Fori(0, (NG - 4) // 2) as r:
                for u in range(2):
                    stage3(2 * r + 3 + u, 2 * r + 1 + u, 1 - u)
            stage3(NG - 1, NG - 3, 1)
            stage3(None, NG - 2, 0)
            stage3(None, NG - 1, 1)

        @block.tensor
        def _(pe):
            pe.wait_ge(S["const_i"], 1)
            pe.wait_ge(S["const_v"], 2)
            pe.wait_ge(S["w_in"], 16 * 9)

            def four(dst, src):
                for b in range(4):
                    last = pe.transpose(dst[:, b * 128:(b + 1) * 128], src(b), ident[:, :])
                return last

            def turn_q(g):
                pe.wait_ge(S["q32_ok"], g + 1)
                pe.wait_ge(S["sq_ok"], g + 1)
                four(psN, lambda b: q32[:, b * 128:(b + 1) * 128]).then_inc(S["n_ps"], 1)

            def stage1(g, u, turn):
                first = isinstance(g, int) and g < 1
                pe.wait_ge(S["xn_ok"], g + 1)
                four(psX, lambda b: xn[:, b * 128:(b + 1) * 128]).then_inc(S["xT_ps"], 1)
                pe.wait_ge(ctx_s[u], 16 * turn)
                four(psC, lambda b: ctx_sb[u][:, b * 128:(b + 1) * 128]).then_inc(S["cT_ps"], 1)
                if not first:
                    turn_q(g - 1)
                pe.wait_ge(S["xT_sb"], g + 1)
                if not first:
                    pe.wait_ge(S["qhi_ok"], g)
                if first:
                    pe.wait_ge(S["wp_ok"], 4)
                pe.matmul(psQ[:, :], wqp[:, :], xT[:, :], start=True, stop=True).then_inc(S["q_ps"], 1)
                pe.wait_ge(S["cT_sb"], g + 1)
                if not first:
                    pe.wait_ge(S["khi_ok"], g)
                pe.matmul(psK[:, :], wkp[:, :], cT[:, :], start=True, stop=True).then_inc(S["k_ps"], 1)
                if not first:
                    pe.wait_ge(S["v_sb"], g)
                for b in range(G):
                    last = pe.matmul(psV[:, b * 128:(b + 1) * 128], cT[:, b * 128:(b + 1) * 128], wv_sb[:, :],
                                     start=True, stop=True)
                last.then_inc(S["v_ps"], 1)

            stage1(0, 0, 1)
            pe.wait_ge(S["w_step"], 2)
            pe.matmul(psW[:, 0:2], ones[:, :], wabs[:, :], start=True, stop=True).then_inc(S["wabs_ps"], 1)

            with pe.Fori(0, (NG - 2) // 2) as r:
                stage1(2 * r + 1, 1, r + 1)
                stage1(2 * r + 2, 0, r + 2)
            stage1(NG - 1, 1, NG // 2)
            turn_q(NG - 1)
            pe.wait_ge(S["norm_ok"], NG + 1)
            for m in range(NSETS):
                pe.transpose(psM[:, m * T:(m + 1) * T], norm_all[:, m * 2 * GH:(m + 1) * 2 * GH], ident[:, :])\
                    .then_inc(S["nT_ps"], 1)
            pe.wait_ge(S["maskT_ok"], 1)
            pe.wait_ge(S["w_step"], 3)
            for m in range(NSETS):
                pe.transpose(psW[:, m * 128:(m + 1) * 128], maskT[:, m, :], ident[:, :]).then_inc(S["m_ps"], 1)

            pe.wait_ge(S["mask_ok"], 1)
            pe.wait_ge(S["ones_in"], 16 * 2 * 2)
            pe.wait_ge(S["w2_in"], 16 * (4 + CT))
            pe.wait_ge(S["sq_ok"], NG + 1)
            pe.wait_ge(S["khi_ok"], NG)
            pe.wait_ge(S["v_sb"], NG)
            pe.wait_ge(S["const_v"], 3)

            def s_unit(s, j, n):
                b, half, q4 = n // 4, n % 2, n % 4 // 2
                N = UNITS * s + n
                if not (isinstance(s, int) and s == 0 and n < SRING):
                    pe.wait_ge(S["max_ok"], N - SRING + 1)
                dst = sbank[(UNITS * j + n) % SRING]
                for i in range(4):
                    k = 4 * q4 + i
                    yield pe.matmul(dst[:, i * T:(i + 1) * T], qop[j][half][0:KS, k, b * T:(b + 1) * T],
                                    kop[j][0:KS, k, b * T:(b + 1) * T], start=True, stop=True)

            def t_unit(t, j, n):
                b, half, q4 = n // 4, (n + 1) % 2, n % 4 // 2
                N = UNITS * t + n
                if not (isinstance(t, int) and t == 0 and n < TRING):
                    pe.wait_ge(S["exp_ok"], N - TRING + 1)
                if n % 8 == 0:
                    pe.wait_ge(nm_in[b // 2], 64 * (t + 1))
                for i in range(4):
                    k = 4 * q4 + i
                    yield pe.matmul(tbank[n % TRING][:, i * T:(i + 1) * T], kop[j][0:KT, k, b * T:(b + 1) * T],
                                    qop[j][half][0:KT, k, b * T:(b + 1) * T], start=True, stop=True)

            def pv_of(t, j, n):
                b, half, q4 = n // 4, (n + 1) % 2, n % 4 // 2
                if n == 0:
                    pe.wait_ge(S["v_ok"], t + 1)
                pe.wait_ge(S["exp_ok"], UNITS * t + n + 1)
                if n % 4 == 0 and not (isinstance(t, int) and t == 0 and n == 0):
                    pe.wait_ge(S["cU_ok"], 4 * t + b)
                w = 2 * half + q4
                for i in range(4):
                    h = HP * half + 4 * q4 + i
                    last = pe.matmul(pvbank[32 * i:32 * i + VW, w * T:(w + 1) * T], vop[j][:, b * H + h, :],
                                     probs[(UNITS * j + n) % PRING][:, i * T:(i + 1) * T], start=True, stop=True)
                last.then_inc(S["pv_unit"], 1)

            def natural(beta):
                pe.wait_ge(S["cU_ok"], beta + 1)
                pe.wait_ge(S["ctxn_ok"], beta)
                four(natbank, lambda w: ctxU[:, w * T:(w + 1) * T]).then_inc(S["nat_ps"], 1)

            def turn_max(sbatch, b):
                pe.wait_ge(S["max_ok"], 4 * (sbatch + 1))
                pe.transpose(nmbank[0:H, 0:T], negmax[b % 2][:, :], ident[:, :]).then_inc(S["nm_ps"], 1)

            def turn_ctx(beta):
                pe.wait_ge(S["ctxn_ok"], beta + 1)
                pe.transpose(mbank[:, 0:T], ctxn[:, :, :].rearrange("p h d -> p (h d)"), ident[:, :])\
                    .then_inc(S["cT2_ps"], 1)

            def project(beta):
                pe.wait_ge(S["cT2_sb"], beta + 1)
                pe.matmul(mbank[:, 0:D], ctxT[:, :], wo_sb[:, :], start=True, stop=True).then_inc(S["proj_ps"], 1)

            def attend(s, sj, t, tj, beside={}):
                tfirst = t is None or (isinstance(t, int) and t == 0)
                if s is not None:
                    if isinstance(s, int):
                        loads = s // NBUF
                    else:
                        loads = s_loads(s, sj)
                    pe.wait_ge(op_in[sj], 16 * LOADS * (loads + 1))
                for n in range(UNITS):
                    su = s_unit(s, sj, n) if s is not None else None
                    tu = t_unit(t, tj, n) if t is not None else None
                    for i in range(4):
                        if su is not None:
                            ms = next(su)
                        if tu is not None:
                            mt = next(tu)
                    if su is not None:
                        ms.then_inc(S["s_done"], 1)
                    if tu is not None:
                        mt.then_inc(S["t_done"], 1)
                    i, bt = n % 4, (4 * t if t is not None else 0) + n // 4
                    if t is not None:
                        if i == 0 and not (tfirst and n == 0):
                            if n > 0:
                                pv_of(t, tj, n - 1)
                            else:
                                pv_of(t - 1, (tj - 1) % NBUF, UNITS - 1)
                        if i == 1 and not (tfirst and n < 8):
                            if not (tfirst and n < 12):
                                pe.wait_ge(S["x1_ok"], bt - 2)
                            turn_ctx(bt - 2)
                        if i == 2 and not (tfirst and n < 4):
                            natural(bt - 1)
                        if i == 2:
                            pv_of(t, tj, n - 2)
                            pv_of(t, tj, n - 1)
                        if i == 3:
                            if not (tfirst and n < 8):
                                project(bt - 2)
                            pv_of(t, tj, n - 1)
                    if i == 1:
                        sbatch = (4 * s if s is not None else 4 * NG) + n // 4 - 1
                        if (s is not None or n == 1) and not (isinstance(s, int) and s == 0 and n < 4):
                            if not (isinstance(s, int) and s == 0 and n < 8):
                                pe.wait_ge(S["nm_ok"], sbatch)
                            turn_max(sbatch, (n // 4 - 1) % 4)
                    if n in beside:
                        beside[n]()

            attend(0, 0, None, None)
            attend(1, 1, 0, 0)
            with pe.Fori(0, 2) as r:
                s_loads = lambda s, sj: r + (1 if sj != 2 else 0)
                for j in range(3):
                    attend(3 * r + 2 + j, (2 + j) % NBUF, 3 * r + 1 + j, (1 + j) % NBUF)

            def weights(i):
                if i >= 2:
                    pe.wait_ge(S["w_sb"], i - 1)
                src = (lambda c: wtap[:, c, i, :]) if i < TAPS else (lambda c: w2_n[:, c * 128:(c + 1) * 128])
                four(bank[i % 2], src).then_inc(S["wtr_ps"], 1)

            pe.wait_ge(S["max_ok"], UNITS * NG)
            pe.wait_ge(S["wtap_ok"], CT * TAPS)
            attend(None, None, 7, 1, {0: lambda: weights(0), 1: lambda: weights(1), 4: lambda: weights(2),
                                      5: lambda: weights(3)})
            pv_of(7, 1, UNITS - 1)
            pe.wait_ge(S["x1_ok"], 4 * NG - 2)
            turn_ctx(4 * NG - 2)
            natural(4 * NG - 1)
            project(4 * NG - 2)
            pe.wait_ge(S["x1_ok"], 4 * NG - 1)
            turn_ctx(4 * NG - 1)
            project(4 * NG - 1)

            pe.wait_ge(S["exp_ok"], UNITS * NG)
            pe.wait_ge(S["w_sb"], TAPS + 1)
            pe.wait_ge(S["x1_ok"], 4 * NG)
            pe.wait_ge(S["ctxn_ok"], 4 * NG)

            def second(m):
                pe.wait_ge(S["zi_ok"], m + 1)
                if not (isinstance(m, int) and m < 1):
                    pe.wait_ge(S["o_ok"], m)
                for b in range(G):
                    for c in range(CT):
                        last = pe.matmul(obank[:, b * D:(b + 1) * D], zi[:, c, b * T:(b + 1) * T], w2t[:, c, :],
                                         start=(c == 0), stop=(c == CT - 1))
                last.then_inc(S["o_ps"], 1)

            def stage3(f, fu, k, ku, m):
                def conv(c):
                    if not (isinstance(f, int) and f < 1 and c < 2):
                        pe.wait_ge(S["z_ok"], CT * f + c - 1)
                    for tap in range(TAPS):
                        last = pe.matmul(ybank[c % 2][:, :], w1t[:, c, tap, :], xqT[:, :, tap:tap + T],
                                         start=(tap == 0), stop=(tap == TAPS - 1))
                    last.then_inc(S["y_ps"], 1)

                def turn_z(b):
                    if not (isinstance(k, int) and k < 1 and b < 2):
                        pe.wait_ge(S["zmax_ok"], G * k + b - 1)
                    four(ztbank[b % 2], lambda c: z[ku][:, c, b * T:(b + 1) * T]).then_inc(S["zt_ps"], 1)

                if f is not None:
                    pe.wait_ge(S["xq_ok"], f + 1)
                    four(xqbank, lambda b: xn[:, b * 128:(b + 1) * 128]).then_inc(S["xqT_ps"], 1)
                if m is not None:
                    second(m)
                if k is not None:
                    pe.wait_ge(S["z_ok"], CT * (k + 1))
                    turn_z(0)
                    turn_z(1)
                if f is not None:
                    pe.wait_ge(S["xqT_sb"], f + 1)
                    conv(0)
                if k is not None:
                    turn_z(2)
                    turn_z(3)
                if f is not None:
                    conv(1)
                if k is not None:
                    pe.wait_ge(S["diag_ok"], k + 1)
                    for b in range(G):
                        last = pe.matmul(scbank[:, b * T:(b + 1) * T], ones[:, :], diag[:, b, :], start=True, stop=True)
                    last.then_inc(S["sc_ps"], 1)
                if f is not None:
                    conv(2)
                    conv(3)
            stage3(0, 0, None, None, None)
            stage3(1, 1, 0, 0, None)
            stage3(2, 0, 1, 1, 0)
            with pe.Fori(0, (NG - 4) // 2) as r:
                for u in range(2):
                    stage3(2 * r + 3 + u, 1 - u, 2 * r + 2 + u, u, 2 * r + 1 + u)
            stage3(NG - 1, 1, NG - 2, 0, NG - 3)
            stage3(None, None, NG - 1, 1, NG - 2)
            second(NG - 1)


_INS = ["x", "ctx_1024", "L0_xattn_Wq", "L0_xattn_bq", "L0_xattn_Wk", "L0_xattn_bk", "L0_xattn_Wv", "L0_xattn_bv",
        "L0_xattn_Wo", "L0_xattn_bo", "L0_ffn_w1", "L0_ffn_conv_w", "L0_ffn_conv_b", "L0_ffn_w2"]


def kernel(**inputs):
    import numpy as _np
    import concourse.bacc as _bacc
    from concourse import mybir as _mybir
    from concourse.bass_utils import run_bass_kernel_spmd as _run

    nc = _bacc.Bacc("TRN2", target_bir_lowering=False, num_devices=1)
    arrays, args = {}, []
    for name in _INS:
        a = _np.ascontiguousarray(inputs[name])
        arrays[f"in_{name}_dram"] = a
        args.append(nc.dram_tensor(f"in_{name}_dram", a.shape, _mybir.dt.from_np(a.dtype), kind="ExternalInput").ap())
    args.append(nc.dram_tensor("out_0_dram", inputs["x"].shape, _mybir.dt.float32, kind="ExternalOutput").ap())
    xattn_ffn_kernel(nc, *args)
    r = _run(nc, [arrays], core_ids=[0])
    return r.results[0]["out_0_dram"]
```
